# Optimizing a Trainium2 kernel written in Bass

```python
import numpy as np
import jax
import jax.numpy as jnp

def _softmax(x, axis=-1):
    return jax.nn.softmax(x, axis=axis)

def _gelu(x):
    return jax.nn.gelu(x, approximate=True)

def _silu(x):
    return jax.nn.silu(x)

def _sigmoid(x):
    return jax.nn.sigmoid(x)

def _layernorm(x, axis=-1, eps=1e-05):
    m = jnp.mean(x, axis=axis, keepdims=True)
    v = jnp.var(x, axis=axis, keepdims=True)
    return (x - m) / jnp.sqrt(v + eps)

def _scatter_add(tgt, idx, src, axis=0):
    return tgt.at[idx].add(src)

def _segment_sum(src, seg, n):
    return jax.ops.segment_sum(src, seg, n)
kernel_name = 'mk_seq_preln_d2_jaxref_r4_4008fd'

def setup_inputs(seed: int=0):
    np.random.seed(seed)
    _w = jnp.asarray

    def _L0_attn_setup():
        import jax, jax.numpy as jnp
        import numpy as np
        D_MODEL = 256
        NUM_HEADS = 16
        HEAD_DIM = D_MODEL // NUM_HEADS
        CURVATURE = 1.0

        def _hyperbolic_distance(q, k, c):
            q_norm_sq = jnp.sum(q * q, axis=-1, keepdims=True)
            k_norm_sq = jnp.sum(k * k, axis=-1)[..., None, :]
            qk = jnp.einsum('bhnd,bhmd->bhnm', q, k)
            diff_sq = q_norm_sq + k_norm_sq - 2.0 * qk
            denom = (1.0 - c * q_norm_sq) * (1.0 - c * k_norm_sq)
            denom = jnp.maximum(denom, 1e-06)
            cosh_arg = 1.0 + 2.0 * c * diff_sq / denom
            cosh_arg = jnp.maximum(cosh_arg, 1.0)
            return jnp.arccosh(cosh_arg)
        key = jax.random.key(seed)
        kx, kq, kk, kv, ko = jax.random.split(key, 5)
        B, N = (2, 512)
        s = 1.0 / np.sqrt(D_MODEL)
        return {'x': jax.random.normal(kx, (B, N, D_MODEL), dtype=jnp.float32), 'wq': jax.random.normal(kq, (D_MODEL, D_MODEL), dtype=jnp.float32) * s, 'wk': jax.random.normal(kk, (D_MODEL, D_MODEL), dtype=jnp.float32) * s, 'wv': jax.random.normal(kv, (D_MODEL, D_MODEL), dtype=jnp.float32) * s, 'wo': jax.random.normal(ko, (D_MODEL, D_MODEL), dtype=jnp.float32) * s}
    _L0_attn_in = _L0_attn_setup()

    def _L0_ffn_setup():
        import jax, jax.numpy as jnp
        import numpy as np
        B, S, D = (1, 512, 256)
        E, K, F = (64, 8, 192)
        SF = 192
        C = 128
        ROUTED_SCALE = 1.0

        def _moe_forward(x, router_w, w_gate, w_up, w_down, ws_gate_up, ws_down):
            T = x.shape[0]
            logits = x.astype(jnp.float32) @ router_w.T
            probs = jax.nn.softmax(logits, axis=-1)
            topk_w, topk_ids = jax.lax.top_k(probs, K)
            topk_w = topk_w / jnp.sum(topk_w, axis=-1, keepdims=True)
            topk_w = topk_w.astype(x.dtype)
            N = T * K
            flat_e = topk_ids.reshape(-1)
            flat_w = topk_w.reshape(-1)
            tok = jnp.arange(N) // K
            onehot = flat_e[:, None] == jnp.arange(E)[None, :]
            pos = jnp.cumsum(onehot, axis=0)[jnp.arange(N), flat_e] - 1
            valid = pos < C
            idx = jnp.where(valid, flat_e * C + pos, E * C)
            x_buf = jnp.zeros((E * C + 1, x.shape[1]), x.dtype).at[idx].set(x[tok])
            xb = x_buf[:E * C].reshape(E, C, -1)
            g = jnp.einsum('ecd,edf->ecf', xb, w_gate)
            u = jnp.einsum('ecd,edf->ecf', xb, w_up)
            h = jax.nn.silu(g) * u
            y = jnp.einsum('ecf,efd->ecd', h, w_down).reshape(E * C, -1)
            safe = jnp.where(valid, idx, 0)
            contrib = y[safe] * (flat_w * valid.astype(flat_w.dtype))[:, None]
            routed = jax.ops.segment_sum(contrib, tok, num_segments=T)
            routed = routed * ROUTED_SCALE
            gu = x @ ws_gate_up
            sg, su = (gu[:, :SF], gu[:, SF:])
            shared = jax.nn.silu(sg) * su @ ws_down
            return routed + shared
        key = jax.random.key(seed)
        ks = jax.random.split(key, 7)
        w = 0.02
        return {'hidden_states': jax.random.normal(ks[0], (B, S, D), jnp.float32), 'router_w': jax.random.normal(ks[1], (E, D), jnp.float32) * w, 'w_gate': jax.random.normal(ks[2], (E, D, F), jnp.float32) * w, 'w_up': jax.random.normal(ks[3], (E, D, F), jnp.float32) * w, 'w_down': jax.random.normal(ks[4], (E, F, D), jnp.float32) * w, 'ws_gate_up': jax.random.normal(ks[5], (D, 2 * SF), jnp.float32) * w, 'ws_down': jax.random.normal(ks[6], (SF, D), jnp.float32) * w}
    _L0_ffn_in = _L0_ffn_setup()

    def _L1_attn_setup():
        import jax, jax.numpy as jnp
        import numpy as np
        B, T = (4, 512)
        D_MODEL = 256
        N_HEADS = 8
        HEAD_DIM = 64
        KV_LRANK = 64

        def _orthogonalize_per_head(w):
            chunks = w.reshape(N_HEADS, HEAD_DIM, D_MODEL)

            def ns(m):
                A = m @ m.T
                Bm = 1.5 * jnp.eye(HEAD_DIM, dtype=m.dtype) - 0.5 * A
                return Bm @ m
            return jax.vmap(ns)(chunks).reshape(w.shape)
        key = jax.random.key(seed)
        ks = jax.random.split(key, 6)

        def lin(k, out_dim, in_dim):
            bound = 1.0 / np.sqrt(in_dim)
            return jax.random.uniform(k, (out_dim, in_dim), jnp.float32, -bound, bound)
        Wq = _orthogonalize_per_head(lin(ks[0], N_HEADS * HEAD_DIM, D_MODEL))
        return {'x': jax.random.normal(ks[1], (B, T, D_MODEL), jnp.float32), 'Wq': Wq, 'Wkv_down': lin(ks[2], KV_LRANK, D_MODEL), 'Wk_up': lin(ks[3], N_HEADS * HEAD_DIM, KV_LRANK), 'Wv_up': lin(ks[4], N_HEADS * HEAD_DIM, KV_LRANK), 'Wo': lin(ks[5], D_MODEL, N_HEADS * HEAD_DIM)}
    _L1_attn_in = _L1_attn_setup()

    def _L1_ffn_setup():
        import jax, jax.numpy as jnp
        import numpy as np
        B, T, D = (4, 512, 256)
        H, DH, E, SEL = (8, 64, 5, 2)

        def _topk_mask(logits, k):
            _, idx = jax.lax.top_k(logits, k)
            return jnp.sum(jax.nn.one_hot(idx, logits.shape[-1], dtype=logits.dtype), axis=-2)
        key = jax.random.key(seed)
        ks = jax.random.split(key, 7)
        s = 0.02
        x = jax.random.normal(ks[0], (B, T, D), dtype=jnp.float32)
        Wq = jax.random.normal(ks[1], (D, H * DH), dtype=jnp.float32) * s
        Wk = jax.random.normal(ks[2], (D, H * DH), dtype=jnp.float32) * s
        Ws = jax.random.normal(ks[3], (D, H * E), dtype=jnp.float32) * s
        Wd = jax.random.normal(ks[4], (D, H * E), dtype=jnp.float32) * s
        Wv = jax.random.normal(ks[5], (E, D, DH), dtype=jnp.float32) * s
        Wo = jax.random.normal(ks[6], (E, DH, D), dtype=jnp.float32) * s
        return {'x': x, 'Wq': Wq, 'Wk': Wk, 'Ws': Ws, 'Wd': Wd, 'Wv': Wv, 'Wo': Wo}
    _L1_ffn_in = _L1_ffn_setup()
    _d = {'L0_attn_x': _L0_attn_in['x'], 'L0_attn_wq': _L0_attn_in['wq'], 'L0_attn_wk': _L0_attn_in['wk'], 'L0_attn_wv': _L0_attn_in['wv'], 'L0_attn_wo': _L0_attn_in['wo'], 'L0_ffn_router_w': _L0_ffn_in['router_w'], 'L0_ffn_w_gate': _L0_ffn_in['w_gate'], 'L0_ffn_w_up': _L0_ffn_in['w_up'], 'L0_ffn_w_down': _L0_ffn_in['w_down'], 'L0_ffn_ws_gate_up': _L0_ffn_in['ws_gate_up'], 'L0_ffn_ws_down': _L0_ffn_in['ws_down'], 'L1_attn_Wq': _L1_attn_in['Wq'], 'L1_attn_Wkv_down': _L1_attn_in['Wkv_down'], 'L1_attn_Wk_up': _L1_attn_in['Wk_up'], 'L1_attn_Wv_up': _L1_attn_in['Wv_up'], 'L1_attn_Wo': _L1_attn_in['Wo'], 'L1_ffn_Wq': _L1_ffn_in['Wq'], 'L1_ffn_Wk': _L1_ffn_in['Wk'], 'L1_ffn_Ws': _L1_ffn_in['Ws'], 'L1_ffn_Wd': _L1_ffn_in['Wd'], 'L1_ffn_Wv': _L1_ffn_in['Wv'], 'L1_ffn_Wo': _L1_ffn_in['Wo']}
    _x0 = _d['L0_attn_x']
    _d['L0_attn_x'] = jax.random.normal(jax.random.fold_in(jax.random.key(seed), 1), (8, 512, 256), dtype=_x0.dtype)
    del _x0
    return _d

def reference(L0_attn_x, L0_attn_wq, L0_attn_wk, L0_attn_wv, L0_attn_wo, L0_ffn_router_w, L0_ffn_w_gate, L0_ffn_w_up, L0_ffn_w_down, L0_ffn_ws_gate_up, L0_ffn_ws_down, L1_attn_Wq, L1_attn_Wkv_down, L1_attn_Wk_up, L1_attn_Wv_up, L1_attn_Wo, L1_ffn_Wq, L1_ffn_Wk, L1_ffn_Ws, L1_ffn_Wd, L1_ffn_Wv, L1_ffn_Wo):

    def _L0_attn_ref(x, wq, wk, wv, wo):
        import jax, jax.numpy as jnp
        import numpy as np
        D_MODEL = 256
        NUM_HEADS = 16
        HEAD_DIM = D_MODEL // NUM_HEADS
        CURVATURE = 1.0

        def _hyperbolic_distance(q, k, c):
            q_norm_sq = jnp.sum(q * q, axis=-1, keepdims=True)
            k_norm_sq = jnp.sum(k * k, axis=-1)[..., None, :]
            qk = jnp.einsum('bhnd,bhmd->bhnm', q, k)
            diff_sq = q_norm_sq + k_norm_sq - 2.0 * qk
            denom = (1.0 - c * q_norm_sq) * (1.0 - c * k_norm_sq)
            denom = jnp.maximum(denom, 1e-06)
            cosh_arg = 1.0 + 2.0 * c * diff_sq / denom
            cosh_arg = jnp.maximum(cosh_arg, 1.0)
            return jnp.arccosh(cosh_arg)
        B, N, D = x.shape
        H, Dh = (NUM_HEADS, HEAD_DIM)
        q = (x @ wq.T).reshape(B, N, H, Dh).transpose(0, 2, 1, 3)
        k = (x @ wk.T).reshape(B, N, H, Dh).transpose(0, 2, 1, 3)
        v = (x @ wv.T).reshape(B, N, H, Dh).transpose(0, 2, 1, 3)
        dist = _hyperbolic_distance(q, k, CURVATURE)
        attn = jax.nn.softmax(-dist, axis=-1)
        out = jnp.einsum('bhnm,bhmd->bhnd', attn, v)
        out = out.transpose(0, 2, 1, 3).reshape(B, N, D)
        return out @ wo.T

    def _L0_ffn_ref(hidden_states, router_w, w_gate, w_up, w_down, ws_gate_up, ws_down):
        import jax, jax.numpy as jnp
        import numpy as np
        B, S, D = (1, 512, 256)
        E, K, F = (64, 8, 192)
        SF = 192
        C = 128
        ROUTED_SCALE = 1.0

        def _moe_forward(x, router_w, w_gate, w_up, w_down, ws_gate_up, ws_down):
            T = x.shape[0]
            logits = x.astype(jnp.float32) @ router_w.T
            probs = jax.nn.softmax(logits, axis=-1)
            topk_w, topk_ids = jax.lax.top_k(probs, K)
            topk_w = topk_w / jnp.sum(topk_w, axis=-1, keepdims=True)
            topk_w = topk_w.astype(x.dtype)
            N = T * K
            flat_e = topk_ids.reshape(-1)
            flat_w = topk_w.reshape(-1)
            tok = jnp.arange(N) // K
            onehot = flat_e[:, None] == jnp.arange(E)[None, :]
            pos = jnp.cumsum(onehot, axis=0)[jnp.arange(N), flat_e] - 1
            valid = pos < C
            idx = jnp.where(valid, flat_e * C + pos, E * C)
            x_buf = jnp.zeros((E * C + 1, x.shape[1]), x.dtype).at[idx].set(x[tok])
            xb = x_buf[:E * C].reshape(E, C, -1)
            g = jnp.einsum('ecd,edf->ecf', xb, w_gate)
            u = jnp.einsum('ecd,edf->ecf', xb, w_up)
            h = jax.nn.silu(g) * u
            y = jnp.einsum('ecf,efd->ecd', h, w_down).reshape(E * C, -1)
            safe = jnp.where(valid, idx, 0)
            contrib = y[safe] * (flat_w * valid.astype(flat_w.dtype))[:, None]
            routed = jax.ops.segment_sum(contrib, tok, num_segments=T)
            routed = routed * ROUTED_SCALE
            gu = x @ ws_gate_up
            sg, su = (gu[:, :SF], gu[:, SF:])
            shared = jax.nn.silu(sg) * su @ ws_down
            return routed + shared
        b, s, d = hidden_states.shape
        x = hidden_states.reshape(-1, d)
        out = _moe_forward(x, router_w, w_gate, w_up, w_down, ws_gate_up, ws_down)
        return out.reshape(b, s, d)

    def _L1_attn_ref(x, Wq, Wkv_down, Wk_up, Wv_up, Wo):
        import jax, jax.numpy as jnp
        import numpy as np
        B, T = (4, 512)
        D_MODEL = 256
        N_HEADS = 8
        HEAD_DIM = 64
        KV_LRANK = 64

        def _orthogonalize_per_head(w):
            chunks = w.reshape(N_HEADS, HEAD_DIM, D_MODEL)

            def ns(m):
                A = m @ m.T
                Bm = 1.5 * jnp.eye(HEAD_DIM, dtype=m.dtype) - 0.5 * A
                return Bm @ m
            return jax.vmap(ns)(chunks).reshape(w.shape)
        b, t, _ = x.shape
        q = (x @ Wq.T).reshape(b, t, N_HEADS, HEAD_DIM)
        kv_latent = x @ Wkv_down.T
        k = (kv_latent @ Wk_up.T).reshape(b, t, N_HEADS, HEAD_DIM)
        v = (kv_latent @ Wv_up.T).reshape(b, t, N_HEADS, HEAD_DIM)
        scale = HEAD_DIM ** (-0.5)
        scores = jnp.einsum('bqhd,bkhd->bhqk', q, k) * scale
        attn = jax.nn.softmax(scores, axis=-1)
        out = jnp.einsum('bhqk,bkhd->bqhd', attn, v)
        out = out.reshape(b, t, N_HEADS * HEAD_DIM)
        return out @ Wo.T

    def _L1_ffn_ref(x, Wq, Wk, Ws, Wd, Wv, Wo):
        import jax, jax.numpy as jnp
        import numpy as np
        B, T, D = (4, 512, 256)
        H, DH, E, SEL = (8, 64, 5, 2)

        def _topk_mask(logits, k):
            _, idx = jax.lax.top_k(logits, k)
            return jnp.sum(jax.nn.one_hot(idx, logits.shape[-1], dtype=logits.dtype), axis=-2)
        e, d, dh = Wv.shape
        h = Wq.shape[1] // dh
        b, t, _ = x.shape
        scale = dh ** (-0.5)
        q = (x @ Wq).reshape(b, t, h, dh).transpose(0, 2, 1, 3)
        k = (x @ Wk).reshape(b, t, h, dh).transpose(0, 2, 1, 3)
        gl_v = (x @ Ws).reshape(b, t, h, e)
        wv = _topk_mask(gl_v, SEL) * jax.nn.sigmoid(gl_v)
        xv = jnp.einsum('btd,edk->btek', x, Wv)
        v = jnp.einsum('bthe,btek->bhtk', wv, xv)
        scores = jnp.einsum('bhid,bhjd->bhij', q * scale, k)
        probs = jax.nn.softmax(scores, axis=-1)
        attn = jnp.einsum('bhij,bhjd->bihd', probs, v)
        gl_o = (x @ Wd).reshape(b, t, h, e)
        mask_o = _topk_mask(gl_o, SEL)
        out = jnp.einsum('bthe,bthk,ekd->btd', mask_o, attn, Wo)
        return out
    x = L0_attn_x
    x = x + _L0_attn_ref(_layernorm(x, axis=-1), L0_attn_wq, L0_attn_wk, L0_attn_wv, L0_attn_wo)
    x = x + _L0_ffn_ref(_layernorm(x, axis=-1), L0_ffn_router_w, L0_ffn_w_gate, L0_ffn_w_up, L0_ffn_w_down, L0_ffn_ws_gate_up, L0_ffn_ws_down)
    x = x + _L1_attn_ref(_layernorm(x, axis=-1), L1_attn_Wq, L1_attn_Wkv_down, L1_attn_Wk_up, L1_attn_Wv_up, L1_attn_Wo)
    x = x + _L1_ffn_ref(_layernorm(x, axis=-1), L1_ffn_Wq, L1_ffn_Wk, L1_ffn_Ws, L1_ffn_Wd, L1_ffn_Wv, L1_ffn_Wo)
    return x

_drawn_inputs = setup_inputs


def setup_inputs(seed=0):
    import zlib

    import numpy as np

    out = dict(_drawn_inputs(seed))
    spreads = {}
    factors = {'L0_attn_wq': 7.966,
     'L0_attn_wk': 6.954,
     'L0_ffn_router_w': 8.0,
     'L0_ffn_w_gate': 8.0,
     'L0_ffn_w_up': 8.0,
     'L0_ffn_w_down': 8.0,
     'L0_ffn_ws_gate_up': 3.845,
     'L0_ffn_ws_down': 3.858,
     'L1_attn_Wq': 7.898,
     'L1_attn_Wkv_down': 4.427,
     'L1_attn_Wk_up': 7.813,
     'L1_attn_Wv_up': 4.21,
     'L1_attn_Wo': 4.145,
     'L1_ffn_Wq': 8.0,
     'L1_ffn_Wk': 8.0,
     'L1_ffn_Ws': 6.127,
     'L1_ffn_Wd': 6.743,
     'L1_ffn_Wv': 3.709,
     'L1_ffn_Wo': 3.695}
    for name, (base, spread) in spreads.items():
        noise = np.random.default_rng([zlib.crc32(name.encode()), seed]).standard_normal(out[name].shape)
        drawn = base * np.exp(spread * noise) if base else spread * noise
        out[name] = jnp.asarray(drawn.astype(out[name].dtype))
    for name, factor in factors.items():
        out[name] = (out[name] * factor).astype(out[name].dtype)
    return out
```

```python
from contextlib import ExitStack

import numpy as np

import concourse.bass as bass
from concourse import mybir

F32 = mybir.dt.float32
F32R = mybir.dt.float32r
BF16 = mybir.dt.bfloat16
I32 = mybir.dt.int32
U32 = mybir.dt.uint32
ALU = mybir.AluOpType
ACT = mybir.ActivationFunctionType
AX = mybir.AxisListType.X

P = 128
B, N, D = 8, 512, 256
T = B * N
NT = N // P
DC = D // P
EPS = 1e-5

H0, DH0 = 16, 16
GH = 4
NG = H0 // GH
QV = DH0 + 2
SL = 64
RING = 2 * GH
CLAMP = 1e-6
SURE = 1e-3

E, K, F, CAP = 64, 8, 192, 128
FC = F - P
ROW = D + E
SLOTS = E * CAP
LOW = -3.0e38

H1, DH1, R1 = 8, 64, 64
C1 = H1 * DH1 // P
SE, SEL = 5, 2
SV = SE * DH1


class Tally:

    def __init__(self, sem):
        self.sem, self.n, self.turn, self.per, self.first = sem, 0, None, 0, 0

    def add(self, n=1, back=0):
        self.n += n
        v = self.n - back
        return v if self.turn is None else self.turn * self.per + v

    def enter(self, turn, per):
        self.turn, self.per, self.first = turn, per, self.n

    def leave(self, turns):
        assert self.n - self.first == self.per, (str(self.sem), self.n - self.first, self.per)
        self.turn, self.n = None, self.first + turns * self.per


class View:

    def __init__(self, sems, per, turns):
        self.sems, self.per, self.turns = sems, per, turns
        self.t, self.turn, self.value = {}, None, None

    def tally(self, name):
        if name not in self.t:
            self.t[name] = Tally(self.sems[name])
            if self.turn is not None:
                self.t[name].enter(self.turn, self.per[name])
        return self.t[name]

    def next(self, name, n=1):
        return self.tally(name).add(n)

    def due(self, name, lag, n=1):
        self.value = self.tally(name).add(n, back=lag)
        return not (isinstance(self.value, int) and self.value <= 0)

    def all_due(self, name):
        return self.due(name, 0, 0)

    def enter(self, turn):
        self.turn = turn
        for name, t in self.t.items():
            t.enter(turn, self.per[name])

    def leave(self):
        self.turn = None
        for t in self.t.values():
            t.leave(self.turns)


WORK_A = DC + 2 * NT + 2 + 4 * NT
WORK_C = NG + DC + NT + DC + 1 + 1 + NT + DC + NT
PER_BATCH = dict(
    x_in=16, res_in=16, var=1, rstd=1, xn=1, signs=1, clamps=1, work=WORK_A + WORK_C,
    work_free=WORK_A + WORK_C, split=NT, scores=2 * H0, scores_free=2 * H0, u=H0, root=H0, w=H0,
    p=H0, pv=H0, o_sb=NG, ao=1, x1=1, var2=1, rstd2=1, xn2=1, mask=1, shifted=1, exps=1,
    weights=1, slots=1, ids_free=1, scattered=16 * NT * K, gu=1, silu=1, hid=1, acc=1,
    xn2_out=16, weights_out=16, acc_out=16,
)


def stage_one(nc, sems, sb, ps, dram, cst, TIDF):
    x_b, xn_b, pw_b, acc_b, table = dram
    TURNS = (B - 2) // 2
    per = {k: 2 * v for k, v in PER_BATCH.items()}

    ident, strict, ones16, onesf, selq, mhalf = (cst[k] for k in ("ident", "strict", "ones16", "onesf", "selq", "mhalf"))
    wqkv, wo, wrt, wgu, wdn = (cst[k] for k in ("wqkv", "wo", "wrt", "wgu", "wdn"))
    eoff, dum, koff = cst["eoff"], cst["dum"], cst["koff"]

    XL = sb("XL", [P, NT, D])
    XN = sb("XN", [P, NT, D])
    XT = sb("XT", [P, DC, N])
    QK = sb("QK", [P, NT, 2 * H0, QV])
    SQ = sb("SQ", [P, NT, 2 * H0 * DH0])
    ST = sb("ST", [P, 2 * H0, SL])
    QT = sb("QT", [P, H0 // 2, N], F32R)
    KT = sb("KT", [P, H0 // 2, N], F32R)
    V = [sb(f"VAL{i}", [P, NT, H0, DH0 + 1]) for i in range(2)]
    TT = sb("TT", [P, RING, NT, N])
    SS = sb("SS", [P, 2, NT, N])
    OS = sb("OS", [P, N])
    AO = sb("AO", [P, NT, D])
    X1 = sb("X1", [P, NT, D])
    XN2 = sb("XN2", [P, NT, D])
    GU = sb("GU", [P, NT, 2 * F])
    LG = sb("LG", [P, NT, E])
    MM = sb("MM", [P, NT, E])
    MK = sb("MK", [P, NT, E])
    MKB = sb("MKB", [P, NT, E], BF16)
    LS = sb("LS", [P, NT, E])
    PW = sb("PW", [P, NT, E])
    V1 = sb("V1", [P, NT, E])
    V2 = sb("V2", [P, NT, E])
    CNT = sb("CNT", [P, E])
    M8 = sb("M8", [P, NT, K])
    K8 = sb("K8", [P, NT, K])
    KO = sb("KO", [P, NT * K])
    IDX = sb("IDX", [P, NT * K], U32)
    TID = sb("TID", [P, NT], U32)
    NR = sb("NR", [P, NT, 2 * H0])
    AM = [sb(f"AM{i}", [P, NT, 2 * H0]) for i in range(2)]
    RR = sb("RR", [P, NT, 2 * H0])
    MX = sb("MX", [P, 2])
    MS = sb("MS", [2, 2])
    SLOW = sb("SLOW", [P, 2])
    SLOWI = [sb(f"SLOWI{i}", [P, 1], I32) for i in range(2)]
    RI = sb("RI", [P, NT, GH])
    stat = [sb(f"stat{i}", [P, NT, 6]) for i in range(2)]
    mv = [sb(f"mv{i}", [P, NT, 2]) for i in range(2)]
    var = [sb(f"var{i}", [P, NT]) for i in range(2)]
    rstd = [sb(f"rstd{i}", [P, NT]) for i in range(2)]
    sm = sb("sm", [P, NT, 2])

    SC = [ps(f"SC{i}", [P, 2, N]) for i in range(2)]
    OB = ps("OB", [P, N])
    NQ = ps("NQ", [P, N])
    WK = [ps(f"WK{i}", [P, N]) for i in range(2)]

    def pipeline(eng, first, step, last):
        v = View(sems, per, TURNS)
        v.items = 0
        first(v)
        for g in range(NG):
            step(v, 0, 0, g, False, True)
        with eng.Fori(0, TURNS) as turn:
            v.enter(turn)
            for half in range(2):
                for g in range(NG):
                    step(v, 2 * turn + 1 + half, (1 + half) % 2, g, True, True)
        v.leave()
        for g in range(NG):
            step(v, B - 1, (B - 1) % 2, g, True, False)
        last(v)

    CARRY = {2: ["norm2", "turn2", "logits", "gate_up"], 3: ["turn", "project01", "project23", "norms"]}
    REST = {2: ["gate_up_rest", "slots", "norm"], 3: ["clamps"]}
    OF_BEFORE = ("norm2", "turn2", "logits", "gate_up", "gate_up_rest", "slots")

    def carry(v, parts, names, par, before, after):
        for name in names:
            if name in parts and (before if name in OF_BEFORE else after):
                parts[name](v, 1 - par)

    def bank_of(v):
        v.items += 1
        return WK[v.items % 2]

    block = nc.Block()
    with block as block:
        @block.sync
        def _(sp):
            def residual(v, b):
                sp.wait_ge(sems["acc_out"], v.next("acc_out", 16))
                sp.dma_start(X1[:], x_b[b]).then_inc(sems["res_in"], 16)

            def store_xn(v, b):
                sp.wait_ge(sems["xn2"], v.next("xn2"))
                sp.dma_start(xn_b[b], XN2[:]).then_inc(sems["xn2_out"], 16)

            def store_rest(v, b):
                sp.wait_ge(sems["weights"], v.next("weights"))
                sp.dma_start(pw_b[b], PW[:]).then_inc(sems["weights_out"], 16)
                sp.wait_ge(sems["acc"], v.next("acc"))
                sp.dma_start(acc_b[b], X1[:]).then_inc(sems["acc_out"], 16)

            def first(v):
                for name in ("acc_out", "xn2_out", "weights_out"):
                    sp.sem_inc(sems[name], 16)
                sp.dma_start(XL[:], x_b[0]).then_inc(sems["x_in"], 16)

            def step(v, b, par, g, before, after):
                if g == 0 and after:
                    sp.wait_ge(sems["xn"], v.next("xn"))
                    sp.dma_start(XL[:], x_b[b + 1]).then_inc(sems["x_in"], 16)
                if g == 0 and before:
                    residual(v, b - 1)
                if g == 2 and before:
                    store_xn(v, b - 1)
                if g == 3 and before:
                    store_rest(v, b - 1)

            def last(v):
                residual(v, B - 1)
                store_xn(v, B - 1)
                store_rest(v, B - 1)
                for name in ("acc_out", "xn2_out", "weights_out"):
                    sp.wait_ge(sems[name], 16 * (B + 1))

            pipeline(sp, first, step, last)

        @block.tensor
        def _(pe):
            def work(v):
                if v.due("work_free", 2):
                    pe.wait_ge(sems["work_free"], v.value)
                return bank_of(v)

            def operands_in(v):
                if v.all_due("work_free"):
                    pe.wait_ge(sems["work_free"], v.value)

            def transposes(v, src, c0, n=P):
                bank = work(v)
                for j in range(NT):
                    ins = pe.transpose(bank[0:n, j * P:(j + 1) * P], src[:, j, c0:c0 + n], ident[:])
                ins.then_inc(sems["work"], 1)

            def product(bank, j, w, n, c0=0):
                for c in range(DC):
                    ins = pe.matmul(bank[:, c0:c0 + n], XT[:, c, j * P:(j + 1) * P], w[:, c, :],
                                    start=(c == 0), stop=(c == DC - 1))
                return ins

            def turn(v, par):
                pe.wait_ge(sems["xn"], v.next("xn"))
                for c in range(DC):
                    transposes(v, XN, c * P)

            def project(j0):
                def run(v, par):
                    operands_in(v)
                    for j in range(j0, j0 + 2):
                        product(work(v), j, wqkv[:, :, 0:2 * D], 2 * D).then_inc(sems["work"], 1)
                        product(work(v), j, wqkv[:, :, 2 * D:3 * D], D).then_inc(sems["work"], 1)
                return run

            def clamps(v, par):
                pe.wait_ge(sems["signs"], v.next("signs"))
                bank = work(v)
                pe.transpose(bank[0:2, 0:P], MX[:], ident[:]).then_inc(sems["work"], 1)
                pe.wait_ge(sems["clamps"], v.next("clamps"))
                bank = work(v)
                pe.matmul(bank[:, 0:2], onesf[0:2, :], MS[:], start=True, stop=True).then_inc(sems["work"], 1)

            def turn_halves(v):
                for j in range(NT):
                    pe.wait_ge(sems["split"], v.next("split"))
                    for side in range(2):
                        for half in range(2):
                            bank = work(v)
                            for r in range(4):
                                h = H0 * side + 2 * (4 * half + r)
                                ins = pe.transpose(bank[:, r * P:(r + 1) * P],
                                                   ST[:, h:h + 2, :].rearrange("p a b -> p (a b)"), ident[:])
                            ins.then_inc(sems["work"], 1)

            def scores(v, h):
                r, pair = SL * (h % 2), h // 2
                for half in range(2):
                    if v.due("scores_free", 2):
                        pe.wait_ge(sems["scores_free"], v.value)
                    for m in range(2):
                        mt = 2 * half + m
                        ins = pe.matmul(SC[half][:, m, :], KT[r:r + 3 * QV, pair, mt * P:(mt + 1) * P],
                                        QT[r:r + 3 * QV, pair, :], start=True, stop=True)
                    if half == 0:
                        ins.then_inc(sems["scores"], 1)
                pe.matmul(NQ[:], selq[r:r + 3 * QV, :], QT[r:r + 3 * QV, pair, :],
                          start=True, stop=True).then_inc(sems["scores"], 1)

            def attend(v, par, h):
                r = 32 * (h % GH)
                if h % GH == 0 and v.due("o_sb", 1):
                    pe.wait_ge(sems["o_sb"], v.value)
                pe.wait_ge(sems["p"], v.next("p"))
                for mt in range(NT):
                    ins = pe.matmul(OB[r:r + DH0 + 1, :], V[par][:, mt, h, :], TT[:, h % RING, mt, :],
                                    start=(mt == 0), stop=(mt == NT - 1))
                ins.then_inc(sems["pv"], 1)

            def turn_group(v):
                if v.all_due("o_sb"):
                    pe.wait_ge(sems["o_sb"], v.value)
                bank = work(v)
                for j in range(NT):
                    ins = pe.transpose(bank[:, j * P:(j + 1) * P], OS[:, j * P:(j + 1) * P], ident[:])
                ins.then_inc(sems["work"], 1)

            def output(v):
                pe.wait_ge(sems["ao"], v.next("ao"))
                for c in range(DC):
                    transposes(v, AO, c * P)
                operands_in(v)
                for j in range(NT):
                    product(work(v), j, wo, D).then_inc(sems["work"], 1)

            def turn2(v, par):
                pe.wait_ge(sems["xn2"], v.next("xn2"))
                for c in range(DC):
                    transposes(v, XN2, c * P)

            def logits(v, par):
                operands_in(v)
                bank = work(v)
                for j in range(NT):
                    ins = product(bank, j, wrt, E, j * E)
                ins.then_inc(sems["work"], 1)

            def gate_up(j0):
                def run(v, par):
                    for j in range(j0, j0 + 2):
                        product(work(v), j, wgu, 2 * F).then_inc(sems["work"], 1)
                return run

            def slots(v, par):
                pe.wait_ge(sems["mask"], v.next("mask"))
                bank = work(v)
                for j in range(NT + 1):
                    for i in range(min(j + 1, NT)):
                        ins = pe.matmul(bank[:, j * E:(j + 1) * E], strict[:] if i == j else ones16[:],
                                        MKB[:, i, :], start=(i == 0), stop=(i == min(j, NT - 1)))
                ins.then_inc(sems["work"], 1)

            def shared(v):
                pe.wait_ge(sems["hid"], v.next("hid"))
                transposes(v, GU, 0)
                transposes(v, GU, F - P)
                operands_in(v)
                for j in range(NT):
                    bank = work(v)
                    pe.matmul(bank[:, 0:D], XT[:, 0, j * P:(j + 1) * P], wdn[:, 0, :], start=True, stop=False)
                    pe.matmul(bank[:, 0:D], XT[P - FC:P, 1, j * P:(j + 1) * P], wdn[P - FC:P, 1, :],
                              start=False, stop=True).then_inc(sems["work"], 1)

            parts = dict(turn=turn, project01=project(0), project23=project(2), clamps=clamps, turn2=turn2,
                         logits=logits, gate_up=gate_up(0), gate_up_rest=gate_up(2), slots=slots)

            def first(v):
                carry(v, parts, CARRY[3] + REST[3], 1, False, True)
                turn_halves(v)

            def step(v, b, par, g, before, after):
                if g == 0:
                    operands_in(v)
                for i in range(GH):
                    scores(v, GH * g + i)
                    if g >= 2:
                        attend(v, par, GH * (g - 2) + i)
                    elif before:
                        attend(v, 1 - par, GH * (NG + g - 2) + i)
                    if g >= 2:
                        carry(v, parts, [CARRY[g][i]], par, before, after)
                if g >= 2 or before:
                    turn_group(v)
                if g == 1 and before:
                    output(v)
                if g >= 2:
                    carry(v, parts, REST[g], par, before, after)
                if g == 3:
                    if before:
                        shared(v)
                    if after:
                        turn_halves(v)

            def last(v):
                for g in (NG - 2, NG - 1):
                    for i in range(GH):
                        attend(v, (B - 1) % 2, GH * g + i)
                    turn_group(v)
                output(v)
                carry(v, parts, CARRY[2] + REST[2], 0, True, False)
                shared(v)

            pipeline(pe, first, step, last)

        @block.vector
        def _(dve):
            slow = [None, None]

            def stats(v, x, i, name):
                for j in range(NT):
                    dve.bn_stats(stat[i][:, j, :], x[:, j, :])
                dve.drain()
                for j in range(NT):
                    dve.bn_aggr(mv[i][:, j, :], stat[i][:, j, :])
                dve.drain()
                dve.tensor_scalar(var[i][:], mv[i][:, :, 1], EPS, None, ALU.add).then_inc(sems[name], 1)

            def normalise(v, out, x, i, name, ready):
                dve.wait_ge(sems[name], v.next(name))
                for j in range(NT):
                    ins = dve.tensor_scalar(out[:, j, :], x[:, j, :], mv[i][:, j, 0:1], rstd[i][:, j:j + 1],
                                            ALU.subtract, ALU.mult)
                ins.then_inc(sems[ready], 1)

            def evacuate(v, dst, view):
                dve.wait_ge(sems["work"], v.next("work"))
                bank = bank_of(v)
                dve.tensor_copy(dst, view(bank)).then_inc(sems["work_free"], 1)

            def heads(lo, hi):
                return lambda bank: bank[:, lo:hi].rearrange("p (h d) -> p h d", d=DH0)

            def norm(v, par):
                normalise(v, XN, XL, 0, "rstd", "xn")

            def turn(v, par):
                for c in range(DC):
                    evacuate(v, XT[:, c, :], lambda bank: bank[:])

            def project(j0):
                def run(v, par):
                    for j in range(j0, j0 + 2):
                        evacuate(v, QK[:, j, :, 0:DH0], heads(0, 2 * D))
                        evacuate(v, V[par][:, j, :, 0:DH0], heads(0, D))
                return run

            def norms(v, par):
                dve.drain()
                qk = QK[:, :, :, 0:DH0].rearrange("p j h d -> p (j h) d")
                sq = SQ[:].rearrange("p j (h d) -> p (j h) d", d=DH0)
                dve.tensor_tensor(sq, qk, qk, ALU.mult)
                dve.drain()
                dve.tensor_reduce(NR[:].rearrange("p j h -> p (j h)"), sq, AX, ALU.add)
                dve.drain()
                am = AM[par]
                dve.tensor_scalar(am[:], NR[:], -1.0, 1.0, ALU.mult, ALU.add)
                dve.drain()
                flat = am[:].rearrange("p j h -> p (j h)")
                dve.tensor_reduce(MX[:, 0:1], flat, AX, ALU.max)
                dve.tensor_reduce(MX[:, 1:2], flat, AX, ALU.min)
                dve.drain()
                dve.tensor_scalar(MX[:, 1:2], MX[:, 1:2], -1.0, None, ALU.mult).then_inc(sems["signs"], 1)

            def clamps(v, par):
                am = AM[par]
                qk = QK[:, :, :, 0:DH0].rearrange("p j h d -> p (j h) d")
                dve.wait_ge(sems["work"], v.next("work"))
                bank = bank_of(v)
                dve.tensor_reduce(MS[:, 0:1], bank[0:2, 0:P], AX, ALU.max).then_inc(sems["work_free"], 1)
                dve.drain()
                dve.tensor_scalar(MS[:, 1:2], MS[:, 0:1], -SURE, None, ALU.is_gt)
                dve.drain()
                dve.tensor_copy(MS[:, 0:1], MS[:, 1:2]).then_inc(sems["clamps"], 1)
                dve.wait_ge(sems["work"], v.next("work"))
                bank = bank_of(v)
                dve.tensor_scalar(SLOW[:], bank[:, 0:2], 1.5, None, ALU.is_gt).then_inc(sems["work_free"], 1)
                dve.drain()
                dve.tensor_scalar(SLOW[:, 1:2], SLOW[:, 0:1], -1.0, 1.0, ALU.mult, ALU.add)
                dve.tensor_copy(SLOWI[par][:], SLOW[:, 0:1])
                dve.drain()
                dve.tensor_scalar(RR[:], am[:], SLOW[:, 1:2], SLOW[:, 0:1], ALU.mult, ALU.add)
                dve.drain()
                dve.reciprocal(RR[:], RR[:])
                dve.drain()
                q, k = slice(0, H0), slice(H0, 2 * H0)
                dve.tensor_scalar(RR[:, :, k], RR[:, :, k], -4.0, None, ALU.mult)
                dve.drain()
                dve.tensor_tensor(QK[:, :, q, DH0], NR[:, :, q], RR[:, :, q], ALU.mult)
                dve.tensor_copy(QK[:, :, q, DH0 + 1], RR[:, :, q])
                dve.tensor_scalar(QK[:, :, k, DH0], RR[:, :, k], -0.5, None, ALU.mult)
                dve.scalar_tensor_tensor(QK[:, :, k, DH0 + 1], NR[:, :, k], -0.5, RR[:, :, k], ALU.mult, ALU.mult)
                dve.tensor_tensor(qk, qk, RR[:].rearrange("p j h -> p (j h)").unsqueeze(2).to_broadcast([P, NT * 2 * H0, DH0]),
                                  ALU.mult)
                dve.drain()

            def turn_halves(v):
                q, k = slice(0, H0), slice(H0, 2 * H0)
                for j in range(NT):
                    hi_q = ST[:, q, 0:2 * QV].rearrange("p h (c d) -> p h c d", c=2)
                    hi_k = ST[:, k, :][:, :, 0:3 * QV].rearrange("p h (c d) -> p h c d", c=3)[:, :, 0:3:2, :]
                    for part, dst in ((q, hi_q), (k, hi_k)):
                        dve.tensor_copy(dst.bitcast(F32R), QK[:, j, part, :].unsqueeze(2).to_broadcast([P, H0, 2, QV]))
                    dve.drain()
                    dve.tensor_tensor(ST[:, q, 2 * QV:3 * QV], QK[:, j, q, :], ST[:, q, 0:QV], ALU.subtract)
                    dve.tensor_tensor(ST[:, k, QV:2 * QV], QK[:, j, k, :], ST[:, k, 0:QV], ALU.subtract)\
                       .then_inc(sems["split"], 1)
                    for dst in (QT, KT):
                        for half in range(2):
                            evacuate(v, dst[:, 4 * half:4 * half + 4, j * P:(j + 1) * P],
                                     lambda bank: bank[:].rearrange("p (a b) -> p a b", a=4))

            def distances(v, par, h, is_slow):
                tt = TT[:, h % RING]
                if v.due("pv", RING):
                    dve.wait_ge(sems["pv"], v.value)
                if is_slow:
                    aq, den = SQ[:, 0, :], SQ[:, 1, :]
                for half in range(2):
                    dve.wait_ge(sems["scores"], v.next("scores"))
                    if not is_slow:
                        dve.tensor_scalar(tt[:, 2 * half:2 * half + 2, :], SC[half][:], 0.0, None, ALU.max)\
                           .then_inc(sems["scores_free"], 1)
                if is_slow:
                    dve.tensor_scalar(aq, NQ[:], -1.0, 1.0, ALU.mult, ALU.add)
                    dve.drain()
                    for mt in range(NT):
                        dve.tensor_scalar(den, aq, AM[par][:, mt, H0 + h:H0 + h + 1], CLAMP, ALU.mult, ALU.max)
                        dve.drain()
                        dve.reciprocal(den, den)
                        dve.drain()
                        ins = dve.scalar_tensor_tensor(tt[:, mt, :], SC[mt // 2][:, mt % 2, :], 0.0, den,
                                                       ALU.max, ALU.mult)
                        dve.drain()
                        if mt % 2:
                            ins.then_inc(sems["scores_free"], 1)

            def square(v, h):
                if v.due("w", 2):
                    dve.wait_ge(sems["w"], v.value)
                tt, ss = TT[:, h % RING], SS[:, h % 2]
                dve.scalar_tensor_tensor(ss, tt, 2.0, tt, ALU.add, ALU.mult).then_inc(sems["u"], 1)

            def scores(v, par, h):
                if h == 0:
                    slow[par] = dve.value_load(SLOWI[par][0:1, 0:1])
                kept = {k: t.n for k, t in v.t.items()}
                with dve.If(slow[par] > 0):
                    distances(v, par, h, True)
                for k, t in v.t.items():
                    t.n = kept.get(k, 0)
                with dve.Else():
                    distances(v, par, h, False)
                dve.drain()

            def collect(v, g):
                dve.tensor_copy(OS[:], OB[:]).then_inc(sems["o_sb"], 1)
                dve.wait_ge(sems["work"], v.next("work"))
                bank = bank_of(v)
                view = bank[:].rearrange("p (j r d) -> p j r d", j=NT, r=GH)
                dve.reciprocal(RI[:], view[:, :, :, DH0])
                dve.drain()
                out = AO[:].rearrange("p j (h d) -> p j h d", d=DH0)[:, :, GH * g:GH * g + GH, :]
                for j in range(NT):
                    ins = dve.tensor_tensor(out[:, j], view[:, j, :, 0:DH0],
                                            RI[:, j, :].unsqueeze(2).to_broadcast([P, GH, DH0]), ALU.mult)
                ins.then_inc(sems["work_free"], 1)
                if g == NG - 1:
                    dve.drain()
                    dve.sem_inc(sems["ao"], 1)

            def output(v):
                for c in range(DC):
                    evacuate(v, XT[:, c, :], lambda bank: bank[:])
                dve.wait_ge(sems["res_in"], v.next("res_in", 16))
                for j in range(NT):
                    dve.wait_ge(sems["work"], v.next("work"))
                    bank = bank_of(v)
                    dve.tensor_tensor(X1[:, j, :], X1[:, j, :], bank[:, 0:D], ALU.add).then_inc(sems["work_free"], 1)
                dve.drain()
                stats(v, X1, 1, "var2")

            def norm2(v, par):
                dve.wait_ge(sems["xn2_out"], v.next("xn2_out", 16))
                normalise(v, XN2, X1, 1, "rstd2", "xn2")

            def logits(v, par):
                evacuate(v, LG[:], lambda bank: bank[:, 0:NT * E].rearrange("p (j e) -> p j e", e=E))
                dve.drain()
                for j in range(NT):
                    dve.max(M8[:, j, :], LG[:, j, :])
                dve.drain()
                for j in range(NT):
                    dve.match_replace(MM[:, j, :], M8[:, j, :], LG[:, j, :], LOW)
                dve.drain()
                dve.tensor_tensor(MKB[:], LG[:], MM[:], ALU.not_equal).then_inc(sems["mask"], 1)
                dve.tensor_tensor(MK[:], LG[:], MM[:], ALU.not_equal)
                dve.tensor_tensor(LS[:], LG[:], M8[:, :, 0:1].to_broadcast([P, NT, E]), ALU.subtract)\
                   .then_inc(sems["shifted"], 1)

            def gate_up(j0):
                def run(v, par):
                    for j in range(j0, j0 + 2):
                        dve.wait_ge(sems["work"], v.next("work"))
                        bank = bank_of(v)
                        dve.tensor_copy(GU[:, j, :], bank[:, 0:2 * F]).then_inc(sems["work_free"], 1)
                    if j0:
                        dve.drain()
                        dve.sem_inc(sems["gu"], 1)
                return run

            def slots(v, par):
                dve.wait_ge(sems["work"], v.next("work"))
                bank = bank_of(v)
                dve.tensor_tensor(V1[:], bank[:, 0:NT * E].rearrange("p (j e) -> p j e", e=E),
                                  CNT[:].unsqueeze(1).to_broadcast([P, NT, E]), ALU.add)
                dve.drain()
                dve.tensor_tensor(CNT[:], CNT[:], bank[:, NT * E:(NT + 1) * E], ALU.add)\
                   .then_inc(sems["work_free"], 1)
                dve.tensor_scalar(V2[:], V1[:], float(CAP), None, ALU.is_ge)
                dve.drain()
                dve.tensor_tensor(V1[:], V1[:], eoff[:].unsqueeze(1).to_broadcast([P, NT, E]), ALU.add)
                dve.drain()
                dve.tensor_scalar(MM[:], V1[:], -1.0, dum[:, 0:1], ALU.mult, ALU.add)
                dve.drain()
                dve.tensor_tensor(MM[:], MM[:], V2[:], ALU.mult)
                dve.drain()
                dve.tensor_tensor(V1[:], V1[:], MM[:], ALU.add)
                dve.drain()
                dve.tensor_tensor(V1[:], V1[:], MK[:], ALU.mult)
                dve.drain()
                for j in range(NT):
                    dve.max(K8[:, j, :], V1[:, j, :])
                dve.drain()
                k8 = K8[:].rearrange("p j k -> p (j k)")
                dve.scalar_tensor_tensor(KO[:], k8, float(SLOTS), koff[:], ALU.is_gt, ALU.mult)
                dve.drain()
                dve.tensor_tensor(KO[:], KO[:], k8, ALU.add)
                dve.drain()
                dve.wait_ge(sems["ids_free"], v.next("ids_free"))
                dve.tensor_copy(TID[:], TIDF[:])
                dve.drain()
                dve.tensor_scalar(TIDF[:], TIDF[:], float(N), None, ALU.add)
                dve.tensor_scalar(IDX[:], KO[:], -1.0, None, ALU.add)\
                   .then_inc(sems["slots"], 1)

            def shared(v):
                dve.wait_ge(sems["exps"], v.next("exps"))
                dve.wait_ge(sems["weights_out"], v.next("weights_out", 16))
                dve.tensor_tensor(PW[:], LS[:], MK[:], ALU.mult)
                dve.drain()
                dve.tensor_reduce(sm[:, :, 0], PW[:], AX, ALU.add)
                dve.drain()
                dve.reciprocal(sm[:, :, 1], sm[:, :, 0])
                dve.drain()
                dve.tensor_tensor(PW[:], PW[:], sm[:, :, 1:2].to_broadcast([P, NT, E]), ALU.mult)\
                   .then_inc(sems["weights"], 1)
                dve.wait_ge(sems["silu"], v.next("silu"))
                dve.tensor_tensor(GU[:, :, 0:F], GU[:, :, 0:F], GU[:, :, F:2 * F], ALU.mult).then_inc(sems["hid"], 1)
                evacuate(v, XT[:, 0, :], lambda bank: bank[:])
                evacuate(v, XT[:, 1, :], lambda bank: bank[:])
                for j in range(NT):
                    dve.wait_ge(sems["work"], v.next("work"))
                    bank = bank_of(v)
                    dve.tensor_tensor(X1[:, j, :], X1[:, j, :], bank[:, 0:D], ALU.add).then_inc(sems["work_free"], 1)
                dve.drain()
                dve.sem_inc(sems["acc"], 1)

            parts = dict(norm=norm, turn=turn, project01=project(0), project23=project(2), norms=norms, clamps=clamps,
                         norm2=norm2, turn2=turn, logits=logits, gate_up=gate_up(0), gate_up_rest=gate_up(2), slots=slots)

            def first(v):
                dve.memset(CNT[:], 0.0)
                dve.memset(ST[:], 0.0)
                dve.memset(OB[:], 0.0)
                for i in range(2):
                    dve.memset(V[i][:], 1.0)
                dve.drain()
                dve.wait_ge(sems["x_in"], v.next("x_in", 16))
                stats(v, XL, 0, "var")
                norm(v, 0)
                carry(v, parts, CARRY[3] + REST[3], 1, False, True)
                turn_halves(v)

            def step(v, b, par, g, before, after):
                for i in range(GH):
                    scores(v, par, GH * g + i)
                    if i < 2:
                        square(v, GH * g + i)
                    if g >= 2:
                        carry(v, parts, [CARRY[g][i]], par, before, after)
                if g >= 2 or before:
                    collect(v, (g - 2) % NG)
                for i in range(2, GH):
                    square(v, GH * g + i)
                if g == 1:
                    if before:
                        output(v)
                    if after:
                        dve.wait_ge(sems["x_in"], v.next("x_in", 16))
                        stats(v, XL, 0, "var")
                if g >= 2:
                    carry(v, parts, REST[g], par, before, after)
                if g == 3:
                    if before:
                        shared(v)
                    if after:
                        turn_halves(v)

            def last(v):
                dve.wait_ge(sems["pv"], B * H0 - GH)
                collect(v, NG - 2)
                dve.wait_ge(sems["pv"], B * H0)
                collect(v, NG - 1)
                output(v)
                carry(v, parts, CARRY[2] + REST[2], 0, True, False)
                shared(v)

            pipeline(dve, first, step, last)

        @block.scalar
        def _(act):
            def roots(v, g):
                for h in range(GH * g, GH * g + GH):
                    act.wait_ge(sems["u"], v.next("u"))
                    act.activation(SS[:, h % 2], SS[:, h % 2], ACT.Sqrt).then_inc(sems["root"], 1)

            def numerators(v, g):
                for h in range(GH * g, GH * g + GH):
                    act.wait_ge(sems["w"], v.next("w"))
                    act.activation(TT[:, h % RING], TT[:, h % RING], ACT.Ln, bias=1.0)
                    act.drain()
                    act.activation(TT[:, h % RING], TT[:, h % RING], ACT.Exp, scale=-1.0).then_inc(sems["p"], 1)

            def route(v):
                act.wait_ge(sems["shifted"], v.next("shifted"))
                act.activation(LS[:], LS[:], ACT.Exp).then_inc(sems["exps"], 1)
                act.wait_ge(sems["gu"], v.next("gu"))
                act.activation(GU[:, :, 0:F], GU[:, :, 0:F], ACT.Silu).then_inc(sems["silu"], 1)

            def step(v, b, par, g, before, after):
                if g >= 2 or before:
                    act.preload_act_table_set("natural_log_exp_and_others")
                    numerators(v, (g - 2) % NG)
                if g == 3 and before:
                    route(v)
                roots(v, g)

            def last(v):
                act.preload_act_table_set("natural_log_exp_and_others")
                numerators(v, NG - 2)
                numerators(v, NG - 1)
                route(v)

            pipeline(act, lambda v: None, step, last)

        @block.gpsimd
        def _(pool):
            def rsqrt(v, i, name, ready):
                pool.wait_ge(sems[name], v.next(name))
                pool.tensor_tensor(rstd[i][:], var[i][:], mhalf[:], ALU.pow).then_inc(sems[ready], 1)

            def scatter(v):
                pool.wait_ge(sems["slots"], v.next("slots"))
                pool.sem_inc(sems["slots_seen"], 1)
                for j in range(NT):
                    scatter_tile(v, j)

            def scatter_tile(v, j):
                for k in range(K):
                    c = j * K + k
                    pool.indirect_dma_start(table, bass.IndirectOffsetOnAxis(ap=IDX[:, c:c + 1], axis=0),
                                            TID[:, j:j + 1], None).then_inc(sems["scattered"], 16)

            def scattered(v):
                pool.wait_ge(sems["scattered"], v.next("scattered", 16 * NT * K))
                pool.sem_inc(sems["ids_free"], 1)

            def first(v):
                pool.sem_inc(sems["ids_free"], 1)
                rsqrt(v, 0, "var", "rstd")

            def step(v, b, par, g, before, after):
                for i in range(GH):
                    h = GH * g + i
                    pool.wait_ge(sems["root"], v.next("root"))
                    tt = TT[:, h % RING].rearrange("p a b -> p (a b)")
                    ss = SS[:, h % 2].rearrange("p a b -> p (a b)")
                    pool.tensor_tensor(tt, tt, ss, ALU.add).then_inc(sems["w"], 1)
                    if g == 3 and before:
                        if i == 0:
                            pool.wait_ge(sems["slots"], v.next("slots"))
                            pool.sem_inc(sems["slots_seen"], 1)
                        scatter_tile(v, i)
                if g == 1 and before:
                    rsqrt(v, 1, "var2", "rstd2")
                if g == 1 and after:
                    rsqrt(v, 0, "var", "rstd")
                if g == 3 and before:
                    scattered(v)

            def last(v):
                rsqrt(v, 1, "var2", "rstd2")
                scatter(v)
                scattered(v)

            pipeline(pool, first, step, last)


UN = 4
PER_EXPERT = dict(
    added=16, x_tr=1, xe=1, gu_e=1, sg=1, h_e=1, h_tr=1, he=1, y=1, ys=1, idx=1,
)


def stage_two(nc, sems, sb, ps, dram, ident):
    row_d, acc_d, slot_d, w_gu, w_dn = dram
    TURNS = E // UN - 2
    per = {k: UN * v for k, v in PER_EXPERT.items()}
    for u in range(UN):
        per[f"weights_in{u}"], per[f"rows_in{u}"] = 48, 16
    WG = [sb(f"WG{i}", [P, DC, 2 * F]) for i in range(UN)]
    WD = [sb(f"WD{i}", [P, 2, D]) for i in range(UN)]
    XG = [sb(f"XG{i}", [P, ROW]) for i in range(UN)]
    IG = [sb(f"IG{i}", [P, 1], U32) for i in range(UN)]
    IA = [sb(f"IA{i}", [P, 1], U32) for i in range(UN)]
    XE = [sb(f"XE{i}", [P, DC, P]) for i in range(2)]
    SG = [sb(f"SG{i}", [P, F]) for i in range(2)]
    HS = [sb(f"HS{i}", [P, F]) for i in range(2)]
    HE = [sb(f"HE{i}", [P, 2, P]) for i in range(2)]
    YS = [sb(f"YS{i}", [P, D]) for i in range(2)]
    SI = sb("SI", [E, CAP], U32)
    SF = sb("SF", [E, CAP])
    IDS = sb("IDS", [P, E], U32)
    x_ps = [ps(f"x_ps{i}", [P, 512]) for i in range(2)]
    g_ps = [ps(f"g_ps{i}", [P, 512]) for i in range(2)]
    h_ps = [ps(f"h_ps{i}", [P, 512]) for i in range(2)]
    y_ps = [ps(f"y_ps{i}", [P, 512]) for i in range(2)]

    def experts(eng, first, step, last):
        v = View(sems, per, TURNS)
        first(v)
        for e in range(UN):
            step(v, e, e, e > 0, True)
        with eng.Fori(0, TURNS) as turn:
            v.enter(turn)
            for u in range(UN):
                step(v, UN * turn + UN + u, u, True, True)
        v.leave()
        for u in range(UN):
            step(v, E - UN + u, u, True, u < UN - 1)
        last(v)

    with nc.Block() as block:
        @block.sync
        def _(sp):
            def step(v, e, u, before, after):
                if v.due("y", UN):
                    sp.wait_ge(sems["y"], v.value)
                sp.dma_start(WG[u][:], w_gu[e].rearrange("(c p) n -> p c n", p=P)).then_inc(sems[f"weights_in{u}"], 16)
                sp.dma_start(WD[u][:, 0, :], w_dn[e][0:P, :]).then_inc(sems[f"weights_in{u}"], 16)
                sp.dma_start(WD[u][P - FC:P, 1, :], w_dn[e][P:F, :]).then_inc(sems[f"weights_in{u}"], 16)

            sp.dma_start(SI[:], slot_d[0:SLOTS, 0].rearrange("(e s) -> e s", e=E)).then_inc(sems["slots_in"], 16)
            experts(sp, lambda v: None, step, lambda v: None)

        @block.gpsimd
        def _(pool):
            def gather(v, u):
                pool.wait_ge(sems["idx"], v.next("idx"))
                pool.sem_inc(sems["slots_seen"], 1)
                pool.indirect_dma_start(XG[u][:], None, row_d, bass.IndirectOffsetOnAxis(ap=IG[u][:, 0:1], axis=0))\
                    .then_inc(sems[f"rows_in{u}"], 16)

            def add(v, u):
                if v.due("added", 16, 16):
                    pool.wait_ge(sems["added"], v.value)
                pool.sem_inc(sems["slots_seen"], 1)
                pool.wait_ge(sems["ys"], v.next("ys"))
                pool.sem_inc(sems["slots_seen"], 1)
                pool.indirect_dma_start(acc_d, bass.IndirectOffsetOnAxis(ap=IA[u][:, 0:1], axis=0),
                                        YS[u % 2][:], None, compute_op=ALU.add).then_inc(sems["added"], 16)

            def first(v):
                for u in range(UN - 1):
                    gather(v, u)

            def step(v, e, u, before, after):
                if before:
                    add(v, (u - 1) % UN)
                if not isinstance(e, int) or e + UN - 1 < E:
                    gather(v, (u - 1) % UN)

            def last(v):
                add(v, UN - 1)
                pool.wait_ge(sems["added"], 16 * E)

            experts(pool, first, step, last)

        @block.tensor
        def _(pe):
            def turn_x(v, u):
                pe.wait_ge(sems[f"rows_in{u}"], v.next(f"rows_in{u}", 16))
                for c in range(DC):
                    ins = pe.transpose(x_ps[u % 2][:, c * P:(c + 1) * P], XG[u][:, c * P:(c + 1) * P], ident[:])
                ins.then_inc(sems["x_tr"], 1)

            def gate_up(v, u):
                pe.wait_ge(sems["xe"], v.next("xe"))
                pe.wait_ge(sems[f"weights_in{u}"], v.next(f"weights_in{u}", 48))
                for c in range(DC):
                    ins = pe.matmul(g_ps[u % 2][:, 0:2 * F], XE[u % 2][:, c, :], WG[u][:, c, :],
                                    start=(c == 0), stop=(c == DC - 1))
                ins.then_inc(sems["gu_e"], 1)

            def turn_h(v, u):
                pe.wait_ge(sems["h_e"], v.next("h_e"))
                pe.transpose(h_ps[u % 2][:, 0:P], HS[u % 2][:, 0:P], ident[:])
                pe.transpose(h_ps[u % 2][:, P:2 * P], HS[u % 2][:, F - P:F], ident[:]).then_inc(sems["h_tr"], 1)

            def down(v, u):
                pe.wait_ge(sems["he"], v.next("he"))
                if v.due("ys", 2):
                    pe.wait_ge(sems["ys"], v.value)
                pe.matmul(y_ps[u % 2][:, 0:D], HE[u % 2][:, 0, :], WD[u][:, 0, :], start=True, stop=False)
                pe.matmul(y_ps[u % 2][:, 0:D], HE[u % 2][P - FC:P, 1, :], WD[u][P - FC:P, 1, :],
                          start=False, stop=True).then_inc(sems["y"], 1)

            def first(v):
                pe.wait_ge(sems["slots_f"], 1)
                pe.transpose(x_ps[1][:, 0:E], SF[:], ident[0:E, 0:E]).then_inc(sems["slots_t"], 1)
                turn_x(v, 0)

            def step(v, e, u, before, after):
                gate_up(v, u)
                if after:
                    turn_x(v, (u + 1) % UN)
                if before:
                    down(v, (u - 1) % UN)
                turn_h(v, u)

            experts(pe, first, step, lambda v: down(v, UN - 1))

        @block.scalar
        def _(act):
            def step(v, e, u, before, after):
                act.wait_ge(sems["gu_e"], v.next("gu_e"))
                if v.due("h_e", 2):
                    act.wait_ge(sems["h_e"], v.value)
                act.activation(SG[u % 2][:], g_ps[u % 2][:, 0:F], ACT.Silu).then_inc(sems["sg"], 1)
                act.wait_ge(sems["h_tr"], v.next("h_tr"))
                if v.due("y", 2):
                    act.wait_ge(sems["y"], v.value)
                act.activation(HE[u % 2][:].rearrange("p a b -> p (a b)"), h_ps[u % 2][:, 0:2 * P], ACT.Copy)\
                   .then_inc(sems["he"], 1)

            experts(act, lambda v: None, step, lambda v: None)

        @block.vector
        def _(dve):
            def indices(v, dst, e):
                return dve.tensor_copy(dst[:], IDS[:, bass.ds(e, 1)])

            def take_x(v, u):
                dve.wait_ge(sems["x_tr"], v.next("x_tr"))
                dve.tensor_copy(XE[u % 2][:].rearrange("p a b -> p (a b)"), x_ps[u % 2][:, 0:2 * P])\
                   .then_inc(sems["xe"], 1)

            def weigh(v, e, u):
                dve.wait_ge(sems["y"], v.next("y"))
                if v.due("added", 32, 16):
                    dve.wait_ge(sems["added"], v.value)
                dve.tensor_scalar(YS[u % 2][:], y_ps[u % 2][:, 0:D], XG[u][:, bass.ds(D + e, 1)], None,
                                  ALU.mult).then_inc(sems["ys"], 1)

            def first(v):
                dve.wait_ge(sems["slots_in"], 16)
                dve.tensor_copy(SF[:], SI[:]).then_inc(sems["slots_f"], 1)
                dve.wait_ge(sems["slots_t"], 1)
                dve.tensor_copy(IDS[:], x_ps[1][:, 0:E])
                dve.drain()
                for u in range(UN - 1):
                    indices(v, IG[u], u).then_inc(sems["idx"], 1)
                take_x(v, 0)

            def step(v, e, u, before, after):
                indices(v, IA[u], e)
                if not isinstance(e, int) or e + UN - 1 < E:
                    indices(v, IG[(u - 1) % UN], e + UN - 1).then_inc(sems["idx"], 1)
                if after:
                    take_x(v, (u + 1) % UN)
                dve.wait_ge(sems["sg"], v.next("sg"))
                if v.due("h_tr", 2):
                    dve.wait_ge(sems["h_tr"], v.value)
                dve.tensor_tensor(HS[u % 2][:], SG[u % 2][:], g_ps[u % 2][:, F:2 * F], ALU.mult)\
                   .then_inc(sems["h_e"], 1)
                if before:
                    weigh(v, e - 1, (u - 1) % UN)

            experts(dve, first, step, lambda v: weigh(v, E - 1, UN - 1))


UNITS = H1 * NT
OUT_1 = [(c, "turn_out1", c, "D") for c in range(C1)] + [(C1 + j, "product_out1", j, "D") for j in range(NT)] \
    + [(8, "stats", 1, None)]
PREP_2 = [(11, "turn_norm", 0, "D"), (12, "turn_norm", 1, "D"), (13, "gates", 0, "D"), (14, "sigmoid", 0, None)] \
    + [(14 + i, "choose", i, None) for i in range(4)] \
    + [(15 + j, "values_of_experts", j, "D") for j in range(NT)] \
    + [(13 + 2 * i, "queries2", i, "A") for i in range(C1)] + [(21 + 2 * i, "keys2", i, "A") for i in range(C1)] \
    + [(18, "mix_values", 0, None)]
OUT_2 = [(19, "turn_out2", 0, "D"), (20, "turn_out2", 1, "D"), (21, "turn_out2", 2, "D")] \
    + [(23 + 2 * j, "product_out2", j, "D") for j in range(NT)]
PREP_1 = [(0, "stats", 0, None), (4, "turn_norm", 0, "D"), (5, "turn_norm", 1, "D"), (7, "latent", 0, "D")] \
    + [(9 + i, "queries1", i, "AD"[i % 2]) for i in range(C1)] + [(13 + 2 * i, "keys1", i, "AD"[i % 2]) for i in range(C1)] \
    + [(21 + 2 * j, "values1", j, "AD"[j % 2]) for j in range(NT)]
STREAM = [(0, "fetch", 0, None), (31, "hand_over", 0, None)]
EVERY_TURN = OUT_1 + PREP_2 + OUT_2 + PREP_1
D_ITEMS = sum(p[3] == "D" for p in EVERY_TURN)
A_ITEMS = sum(p[3] == "A" for p in EVERY_TURN)
PER_BATCH_1 = dict(
    xl_in=16, xr_in=16, xo_in=16, out_st=16, x4=1, var1=2, normed=2, item_d=D_ITEMS, item_a=A_ITEMS,
    free_d=D_ITEMS, free_a=A_ITEMS, s=2 * UNITS, peak=2 * UNITS, prob=2 * UNITS, turned_d=UNITS, turned_a=UNITS,
    in_d=UNITS, in_a=UNITS, pv_d=UNITS, pv_a=UNITS, head=2 * H1, gl=1, sig=1, wv=1, experts_in=1, vh=H1, gadd=H1,
)


def stage_three(nc, sems, sb, ps, dram, w, ident):
    x_b, out_b = dram
    TURNS = B - 3
    q1, down1, k1, v1 = sb("q1s", [P, DC, H1 * DH1]), sb("down1s", [P, DC, R1]), sb("k1s", [R1, H1 * DH1]), sb("v1s", [R1, H1 * DH1])
    o1, q2, k2 = sb("o1s", [P, C1, D]), sb("q2s", [P, DC, H1 * DH1]), sb("k2s", [P, DC, H1 * DH1])
    g2, v2, o2 = sb("g2s", [P, DC, 2 * H1 * SE]), sb("v2s", [P, DC, SV]), sb("o2s", [P, 3, D])
    mhalf = sb("mhalf1", [P, NT])
    XL = sb("XL1", [P, NT, D])
    XR = sb("XR1", [P, NT, D])
    XO = sb("XO1", [P, NT, D])
    XN = sb("XN1", [P, NT, D])
    XT = sb("XT1", [P, DC, N])
    LT = sb("LT1", [R1, N])
    AT = sb("AT1", [P, C1, N])
    AO = sb("AO1", [P, NT, H1 * DH1])
    AH = [sb(f"AH{i}", [P, NT, DH1]) for i in range(2)]
    GO = sb("GO", [P, NT, SV])
    GT = sb("GT", [P, NT, SV])
    XV = sb("XV", [P, NT, SV])
    QT = {k: sb(f"QT{k}", [P, C1, N]) for k in (1, 2)}
    KT = {k: sb(f"KT{k}", [P, C1, N]) for k in (1, 2)}
    VN = {k: sb(f"VN{k}", [P, NT, H1 * DH1]) for k in (1, 2)}
    VM = [sb(f"VM{i}", [P, NT, DH1]) for i in range(2)]
    PR = [sb(f"PR{i}", [P, N]) for i in range(2)]
    PT = [sb(f"PT{i}", [P, NT, P]) for i in range(2)]
    NM = sb("NM", [P, 2])
    SM = sb("SM", [P, 2, NT])
    RS = sb("RS", [P, NT])
    GL = sb("GL", [P, NT * 2 * H1, SE])
    CN = sb("CN", [P, NT * 2 * H1, SE])
    CM = sb("CM", [P, SE - 1, NT * 2 * H1, SE - 1])
    SIG = sb("SIG", [P, NT, H1, SE])
    WV = sb("WV", [P, NT, H1, SE])
    MO = sb("MO", [P, NT, H1, SE])
    stat = sb("statl1", [P, NT, 6])
    mv = sb("mvl1", [P, NT, 2])
    var = sb("var1b", [P, NT])
    rstd = sb("rstd1b", [P, NT])

    S = [ps(f"S{i}", [P, N]) for i in range(2)]
    TP = [ps(f"TP{i}", [P, N]) for i in range(2)]
    OP = [ps(f"OP{i}", [P, NT, P]) for i in range(2)]
    BD, BA = ps("BD", [P, N]), ps("BA", [P, N])

    loads = [
        (q1[:], w["q1"].rearrange("(c p) n -> p c n", p=P)), (down1[:], w["down1"].rearrange("(c p) n -> p c n", p=P)),
        (k1[:], w["k1"]), (v1[:], w["v1"]), (o1[:], w["o1"].rearrange("(c p) n -> p c n", p=P)),
        (q2[:], w["q2"].rearrange("(c p) n -> p c n", p=P)), (k2[:], w["k2"].rearrange("(c p) n -> p c n", p=P)),
        (g2[:], w["g2"].rearrange("(c p) n -> p c n", p=P)), (v2[:], w["v2"].rearrange("(c p) n -> p c n", p=P)),
        (o2[:, 0:2, :], w["o2"][0:2 * P, :].rearrange("(c p) n -> p c n", p=P)),
        (o2[3 * P - SV:P, 2, :], w["o2"][2 * P:SV, :]),
    ]

    def passes(eng, parts, unit=None, begin=None, end=None, ends_turn=None):
        v = View(sems, PER_BATCH_1, TURNS)

        def carry(b, table, u):
            for at, part, i, reader in table:
                if at == u and part in parts:
                    parts[part](v, i, b)

        def alone(b, table):
            for u in range(UNITS):
                carry(b, table, u)

        def run(kind, before, after, *tables):
            if begin and before is None:
                begin(v, kind)
            for u in range(UNITS):
                if unit:
                    unit(v, kind, u, before, after)
                for b, table in tables:
                    carry(b, table, u)
            if end and after is None:
                end(v, kind)

        alone(0, PREP_1)
        run(1, None, None)
        alone(1, PREP_1)
        run(1, None, 2, (0, OUT_1), (0, PREP_2), (0, STREAM))
        run(2, 1, 1, (2, PREP_1))
        with eng.Fori(0, TURNS) as turn:
            v.enter(turn)
            run(1, 2, 2, (turn + 1, OUT_1), (turn + 1, PREP_2), (turn, OUT_2),
                (turn + 1, STREAM))
            run(2, 1, 1, (turn + 3, PREP_1))
        v.leave()
        run(1, 2, 2, (B - 2, OUT_1), (B - 2, PREP_2), (B - 3, OUT_2), (B - 2, STREAM))
        run(2, 1, None)
        alone(B - 1, OUT_1)
        alone(B - 1, PREP_2)
        alone(B - 2, OUT_2)
        alone(B - 1, STREAM)
        run(2, None, None)
        alone(B - 1, OUT_2)
        return v

    with nc.Block() as block:
        @block.sync
        def _(sp):
            def load_norm(v, b):
                sp.dma_start(XL[:], x_b[b]).then_inc(sems["xl_in"], 16)

            def load_residual(v, b):
                sp.dma_start(XR[:], x_b[b]).then_inc(sems["xr_in"], 16)

            def stats(v, second, b):
                v.tally("normed").add(1)
                if isinstance(b, int) and b == 0 and not second:
                    if v.all_due("normed"):
                        sp.wait_ge(sems["normed"], v.value)
                    load_norm(v, 1)

            def fetch(v, i, b):
                if v.all_due("normed"):
                    sp.wait_ge(sems["normed"], v.value)
                if not isinstance(b, int) or b + 2 < B:
                    load_norm(v, b + 2)

            def hand_over(v, i, b):
                if isinstance(b, int) and b == 0:
                    if v.all_due("normed"):
                        sp.wait_ge(sems["normed"], v.value)
                else:
                    if v.all_due("out_st"):
                        sp.wait_ge(sems["out_st"], v.value)
                sp.dma_start(XO[:], XR[:]).then_inc(sems["xo_in"], 16)
                sp.wait_ge(sems["xo_in"], v.next("xo_in", 16))
                if not isinstance(b, int) or b + 1 < B:
                    load_residual(v, b + 1)

            def store(v, j, b):
                if j < NT - 1:
                    return
                sp.wait_ge(sems["x4"], v.next("x4"))
                sp.dma_start(out_b[b], XO[:]).then_inc(sems["out_st"], 16)
                v.tally("out_st").add(16)

            for dst, src in loads:
                sp.dma_start(dst, src).then_inc(sems["loaded1"], 16)
            sp.dma_start(XL[:], x_b[0]).then_inc(sems["xl_in"], 16)
            sp.dma_start(XR[:], x_b[0]).then_inc(sems["xr_in"], 16)
            v = passes(sp, dict(stats=stats, fetch=fetch, hand_over=hand_over, product_out2=store))
            if v.all_due("out_st"):
                sp.wait_ge(sems["out_st"], v.value)

        @block.tensor
        def _(pe):
            def item(v, reader):
                name = "free_" + reader.lower()
                if v.due(name, 1):
                    pe.wait_ge(sems[name], v.value)
                return BD if reader == "D" else BA

            def operands_in(v):
                if v.all_due("free_d"):
                    pe.wait_ge(sems["free_d"], v.value)
                if v.all_due("free_a"):
                    pe.wait_ge(sems["free_a"], v.value)

            def done(ins, reader):
                ins.then_inc(sems["item_" + reader.lower()], 1)

            def turn_norm(v, c, b):
                if c == 0:
                    pe.wait_ge(sems["normed"], v.next("normed"))
                bank = item(v, "D")
                for j in range(NT):
                    ins = pe.transpose(bank[:, j * P:(j + 1) * P], XN[:, j, c * P:(c + 1) * P], ident[:])
                done(ins, "D")

            def by_width(weight, x, chunks):
                def part(reader_of):
                    def run(v, i, b):
                        operands_in(v)
                        reader = reader_of(i)
                        bank = item(v, reader)
                        for c in range(chunks):
                            ins = pe.matmul(bank[:], weight(c, i), x(c), start=(c == 0), stop=(c == chunks - 1))
                        done(ins, reader)
                    return run
                return part

            def by_token(x, weight, chunks, n, reader_of=lambda j: "D"):
                def run(v, j, b):
                    operands_in(v)
                    reader = reader_of(j)
                    bank = item(v, reader)
                    for c in range(chunks):
                        ins = pe.matmul(bank[:, 0:n], x(c, j), weight(c), start=(c == 0), stop=(c == chunks - 1))
                    done(ins, reader)
                return run

            def both(i):
                return "AD"[i % 2]

            def xt(c):
                return XT[:, c, :]

            def xt_tile(c, j):
                return XT[:, c, j * P:(j + 1) * P]

            def columns(wt):
                return lambda c, i: wt[:, c, i * P:(i + 1) * P]

            def latent(v, i, b):
                operands_in(v)
                bank = item(v, "D")
                for c in range(DC):
                    ins = pe.matmul(bank[0:R1, :], down1[:, c, :], XT[:, c, :], start=(c == 0), stop=(c == DC - 1))
                done(ins, "D")

            def gates(v, i, b):
                operands_in(v)
                bank = item(v, "D")
                n = 2 * H1 * SE
                for j in range(NT):
                    for c in range(DC):
                        ins = pe.matmul(bank[:, j * n:(j + 1) * n], xt_tile(c, j), g2[:, c, :],
                                        start=(c == 0), stop=(c == DC - 1))
                done(ins, "D")

            def turn_out1(v, c, b):
                if c == 0:
                    if v.all_due("head"):
                        pe.wait_ge(sems["head"], v.value)
                bank = item(v, "D")
                for j in range(NT):
                    ins = pe.transpose(bank[:, j * P:(j + 1) * P], AO[:, j, c * P:(c + 1) * P], ident[:])
                done(ins, "D")

            def turn_out2(v, c, b):
                if c == 0:
                    pe.wait_ge(sems["gadd"], v.next("gadd", H1))
                bank = item(v, "D")
                lo = min(c * P, SV - P)
                for j in range(NT):
                    ins = pe.transpose(bank[:, j * P:(j + 1) * P], GO[:, j, lo:lo + P], ident[:])
                done(ins, "D")

            def product_out2(v, j, b):
                operands_in(v)
                bank = item(v, "D")
                for c in range(3):
                    r = 0 if c < 2 else 3 * P - SV
                    ins = pe.matmul(bank[:, 0:D], AT[r:P, c, j * P:(j + 1) * P], o2[r:P, c, :],
                                    start=(c == 0), stop=(c == 2))
                done(ins, "D")

            def scores(v, kind, u):
                h, j = u // NT, u % NT
                r = DH1 * (h % 2)
                if u == 0:
                    operands_in(v)
                pe.matmul(S[u % 2][:], QT[kind][r:r + DH1, h // 2, j * P:(j + 1) * P], KT[kind][r:r + DH1, h // 2, :],
                          start=True, stop=True).then_inc(sems["s"], 1)

            def turn(v, u):
                pe.wait_ge(sems["prob"], v.next("prob"))
                for m in range(NT):
                    ins = pe.transpose(TP[u % 2][:, m * P:(m + 1) * P], PR[u % 2][:, m * P:(m + 1) * P], ident[:])
                ins.then_inc(sems["turned_" + "da"[u % 2]], 1)

            def attend(v, kind, u):
                h, j = u // NT, u % NT
                if j == 0:
                    if v.due("head", 2):
                        pe.wait_ge(sems["head"], v.value)
                    if kind == 2:
                        pe.wait_ge(sems["vh"], v.next("vh"))
                pe.wait_ge(sems["in_" + "da"[u % 2]], v.next("in_" + "da"[u % 2]))
                for m in range(NT):
                    ins = pe.matmul(OP[h % 2][:, j, 0:DH1], PT[u % 2][:, m, :], VN[kind][:, m, h * DH1:(h + 1) * DH1],
                                    start=(m == 0), stop=(m == NT - 1))
                ins.then_inc(sems["pv_" + "da"[u % 2]], 1)

            def begin(v, kind):
                scores(v, kind, 0)
                scores(v, kind, 1)

            def unit(v, kind, u, before, after):
                turn(v, u)
                if u + 2 < UNITS:
                    scores(v, kind, u + 2)
                elif after:
                    scores(v, after, u + 2 - UNITS)
                if u > 0:
                    attend(v, kind, u - 1)
                elif before:
                    attend(v, before, UNITS - 1)

            def end(v, kind):
                attend(v, kind, UNITS - 1)

            pe.wait_ge(sems["loaded1"], 16 * len(loads))
            passes(pe, dict(
                turn_norm=turn_norm, latent=latent, gates=gates, turn_out1=turn_out1, turn_out2=turn_out2,
                product_out2=product_out2,
                queries1=by_width(columns(q1), xt, DC)(both), queries2=by_width(columns(q2), xt, DC)(lambda i: "A"),
                keys1=by_width(lambda c, i: k1[:, i * P:(i + 1) * P], lambda c: LT[:], 1)(both),
                keys2=by_width(columns(k2), xt, DC)(lambda i: "A"),
                values1=by_token(lambda c, j: LT[:, j * P:(j + 1) * P], lambda c: v1[:], 1, H1 * DH1, both),
                values_of_experts=by_token(xt_tile, lambda c: v2[:, c, :], DC, SV),
                product_out1=by_token(lambda c, j: AT[:, c, j * P:(j + 1) * P], lambda c: o1[:, c, :], C1, D),
            ), unit, begin, end)

        @block.scalar
        def _(act):
            def take(dst, scale=1.0, mine=lambda i: i % 2 == 0):
                def run(v, i, b):
                    if not mine(i):
                        return
                    act.wait_ge(sems["item_a"], v.next("item_a"))
                    act.activation(dst(i), BA[:], ACT.Copy, scale=scale).then_inc(sems["free_a"], 1)
                return run

            def sigmoid(v, i, b):
                act.wait_ge(sems["gl"], v.next("gl"))
                act.activation(SIG[:], GL[:].rearrange("p (j s h) e -> p j s h e", j=NT, s=2)[:, :, 0],
                               ACT.Exp, scale=-1.0).then_inc(sems["sig"], 1)

            def numerators(v, u):
                h, j = u // NT, u % NT
                if j == 0:
                    if v.due("head", 2):
                        act.wait_ge(sems["head"], v.value)
                act.wait_ge(sems["peak"], v.next("peak"))
                if u % 2 == 0:
                    if v.due("turned_d", 1):
                        act.wait_ge(sems["turned_d"], v.value)
                act.activation(PR[u % 2][:], S[u % 2][:], ACT.Exp, bias=NM[:, u % 2:u % 2 + 1],
                               accum_out=SM[:, h % 2, j:j + 1]).then_inc(sems["prob"], 1)

            def begin(v, kind):
                numerators(v, 0)

            def unit(v, kind, u, before, after):
                if u + 1 < UNITS:
                    numerators(v, u + 1)
                elif after:
                    numerators(v, 0)
                if u % 2:
                    act.wait_ge(sems["turned_a"], v.next("turned_a"))
                    if v.due("pv_a", 1):
                        act.wait_ge(sems["pv_a"], v.value)
                    act.activation(PT[1][:], TP[1][:].rearrange("p (m n) -> p m n", m=NT), ACT.Copy)\
                       .then_inc(sems["in_a"], 1)

            every = lambda i: True
            passes(act, dict(
                queries1=take(lambda i: QT[1][:, i, :], DH1 ** -0.5), keys1=take(lambda i: KT[1][:, i, :]),
                values1=take(lambda j: VN[1][:, j, :]), sigmoid=sigmoid,
                queries2=take(lambda i: QT[2][:, i, :], DH1 ** -0.5, every), keys2=take(lambda i: KT[2][:, i, :], 1.0, every),
            ), unit, begin)

        @block.vector
        def _(dve):
            def take(dst, src=lambda: BD[:], scale=None, mine=lambda i: True):
                def run(v, i, b):
                    if not mine(i):
                        return
                    dve.wait_ge(sems["item_d"], v.next("item_d"))
                    if scale is None:
                        ins = dve.tensor_copy(dst(i), src())
                    else:
                        ins = dve.tensor_scalar(dst(i), src(), scale, None, ALU.mult)
                    ins.then_inc(sems["free_d"], 1)
                return run

            def stats(v, second, b):
                x = XR if second else XL
                if not second:
                    dve.wait_ge(sems["xl_in"], v.next("xl_in", 16))
                if v.due("normed", 1):
                    dve.wait_ge(sems["normed"], v.value)
                for j in range(NT):
                    dve.bn_stats(stat[:, j, :], x[:, j, :])
                dve.drain()
                for j in range(NT):
                    dve.bn_aggr(mv[:, j, :], stat[:, j, :])
                dve.drain()
                dve.tensor_scalar(var[:], mv[:, :, 1], EPS, None, ALU.add).then_inc(sems["var1"], 1)

            def product_out1(v, j, b):
                if j == 0:
                    dve.wait_ge(sems["xr_in"], v.next("xr_in", 16))
                dve.wait_ge(sems["item_d"], v.next("item_d"))
                dve.tensor_tensor(XR[:, j, :], XR[:, j, :], BD[:, 0:D], ALU.add).then_inc(sems["free_d"], 1)
                if j == NT - 1:
                    dve.drain()

            def product_out2(v, j, b):
                if j == 0:
                    dve.wait_ge(sems["xo_in"], v.next("xo_in", 16))
                dve.wait_ge(sems["item_d"], v.next("item_d"))
                dve.tensor_tensor(XO[:, j, :], XO[:, j, :], BD[:, 0:D], ALU.add).then_inc(sems["free_d"], 1)
                if j == NT - 1:
                    dve.drain()
                    dve.sem_inc(sems["x4"], 1)

            def gates(v, i, b):
                dve.wait_ge(sems["item_d"], v.next("item_d"))
                dve.tensor_copy(GL[:].rearrange("p a e -> p (a e)"), BD[:, 0:NT * 2 * H1 * SE]).then_inc(sems["free_d"], 1)
                dve.drain()
                dve.sem_inc(sems["gl"], 1)

            def values_of_experts(v, j, b):
                if j == 0 and v.all_due("vh"):
                    dve.wait_ge(sems["vh"], v.value)
                dve.wait_ge(sems["item_d"], v.next("item_d"))
                dve.tensor_copy(XV[:, j, :], BD[:, 0:SV]).then_inc(sems["free_d"], 1)
                if j == NT - 1:
                    dve.drain()
                    dve.sem_inc(sems["experts_in"], 1)

            def choose(v, i, b):
                if i == 0:
                    for e in range(SE):
                        dve.memset(CN[:, :, e:e + 1], float(SE - 1 - e))
                    for s in range(1, SE):
                        dve.tensor_tensor(CM[:, s - 1, :, 0:SE - s], GL[:, :, 0:SE - s], GL[:, :, s:SE], ALU.is_ge)
                    dve.drain()
                if i in (1, 2):
                    for s in (2 * i - 1, 2 * i):
                        dve.tensor_tensor(CN[:, :, s:SE], CN[:, :, s:SE], CM[:, s - 1, :, 0:SE - s], ALU.add)
                        dve.drain()
                        dve.tensor_tensor(CN[:, :, 0:SE - s], CN[:, :, 0:SE - s], CM[:, s - 1, :, 0:SE - s], ALU.subtract)
                        dve.drain()
                if i == 2:
                    dve.wait_ge(sems["sig"], v.next("sig"))
                    dve.tensor_scalar(SIG[:], SIG[:], 1.0, None, ALU.add)
                    dve.drain()
                if i == 3:
                    count = CN[:].rearrange("p (j s h) e -> p j s h e", j=NT, s=2)
                    if v.due("vh", H1, H1):
                        dve.wait_ge(sems["vh"], v.value)
                    if v.all_due("gadd"):
                        dve.wait_ge(sems["gadd"], v.value)
                    dve.tensor_scalar(MO[:], count[:, :, 1], float(SEL), None, ALU.is_lt)
                    dve.reciprocal(SIG[:], SIG[:])
                    dve.drain()
                    dve.scalar_tensor_tensor(WV[:], count[:, :, 0], float(SEL), SIG[:], ALU.is_lt, ALU.mult)\
                       .then_inc(sems["wv"], 1)

            def peak(v, u):
                dve.wait_ge(sems["s"], v.next("s"))
                dve.tensor_reduce(NM[:, u % 2:u % 2 + 1], S[u % 2][:], AX, ALU.max, negate=True)\
                   .then_inc(sems["peak"], 1)

            def close(v, kind, h):
                dve.wait_ge(sems["pv_a"], v.next("pv_a", NT // 2))
                dve.reciprocal(RS[:], SM[:, h % 2, :])
                dve.drain()
                if kind == 2:
                    if v.due("gadd", 2):
                        dve.wait_ge(sems["gadd"], v.value)
                out = AO[:, :, h * DH1:(h + 1) * DH1] if kind == 1 else AH[h % 2][:]
                dve.tensor_tensor(out, OP[h % 2][:, :, 0:DH1], RS[:].unsqueeze(2).to_broadcast([P, NT, DH1]), ALU.mult)\
                   .then_inc(sems["head"], 1)

            def begin(v, kind):
                peak(v, 0)

            def unit(v, kind, u, before, after):
                if u + 1 < UNITS:
                    peak(v, u + 1)
                elif after:
                    peak(v, 0)
                if u % 2 == 0:
                    dve.wait_ge(sems["turned_d"], v.next("turned_d"))
                    if v.due("pv_d", 1):
                        dve.wait_ge(sems["pv_d"], v.value)
                    dve.tensor_copy(PT[0][:], TP[0][:].rearrange("p (m n) -> p m n", m=NT)).then_inc(sems["in_d"], 1)
                if u % NT == 0:
                    if u > 0:
                        close(v, kind, u // NT - 1)
                    elif before:
                        close(v, before, H1 - 1)

            def end(v, kind):
                close(v, kind, H1 - 1)

            odd = lambda i: i % 2 == 1
            dve.memset(mhalf[:], -0.5)
            dve.drain()
            dve.sem_inc(sems["primed1"], 1)
            passes(dve, dict(
                stats=stats, turn_norm=take(lambda c: XT[:, c, :]), latent=take(lambda i: LT[:], lambda: BD[0:R1, :]),
                queries1=take(lambda i: QT[1][:, i, :], scale=DH1 ** -0.5, mine=odd),
                keys1=take(lambda i: KT[1][:, i, :], mine=odd), values1=take(lambda j: VN[1][:, j, :], mine=odd),
                turn_out1=take(lambda c: AT[:, c, :]), turn_out2=take(lambda c: AT[:, c, :]),
                product_out1=product_out1, product_out2=product_out2, gates=gates, choose=choose,
                values_of_experts=values_of_experts,
            ), unit, begin, end)

        @block.gpsimd
        def _(pool):
            def stats(v, second, b):
                x = XR if second else XL
                pool.wait_ge(sems["var1"], v.next("var1"))
                pool.tensor_tensor(rstd[:], var[:], mhalf[:], ALU.pow)
                pool.drain()
                for j in range(NT):
                    ins = pool.tensor_scalar(XN[:, j, :], x[:, j, :], mv[:, j, 0:1], rstd[:, j:j + 1],
                                             ALU.subtract, ALU.mult)
                ins.then_inc(sems["normed"], 1)

            def mix_values(v, i, b):
                pool.wait_ge(sems["wv"], v.next("wv"))
                pool.wait_ge(sems["experts_in"], v.next("experts_in"))
                for h in range(H1):
                    for e in range(SE):
                        tmp = VM[e % 2][:] if e else VN[2][:, :, h * DH1:(h + 1) * DH1]
                        pool.tensor_tensor(tmp, XV[:, :, e * DH1:(e + 1) * DH1],
                                           WV[:, :, h, e:e + 1].to_broadcast([P, NT, DH1]), ALU.mult)
                        pool.drain()
                        if e:
                            ins = pool.tensor_tensor(VN[2][:, :, h * DH1:(h + 1) * DH1],
                                                     VN[2][:, :, h * DH1:(h + 1) * DH1], tmp, ALU.add)
                    ins.then_inc(sems["vh"], 1)

            def add_head(v, h):
                pool.drain()
                if h == 0:
                    if v.all_due("x4"):
                        pool.wait_ge(sems["x4"], v.value)
                pool.wait_ge(sems["head"], v.next("head"))
                go = GO[:].rearrange("p j (e d) -> p j e d", e=SE)
                gt = GT[:].rearrange("p j (e d) -> p j e d", e=SE)
                dst = go if h == 0 else gt
                for j in range(NT):
                    ins = pool.tensor_tensor(dst[:, j], AH[h % 2][:, j, :].unsqueeze(1).to_broadcast([P, SE, DH1]),
                                             MO[:, j, h, :].unsqueeze(2).to_broadcast([P, SE, DH1]), ALU.mult)
                if h:
                    pool.drain()
                    ins = pool.tensor_tensor(GO[:], GO[:], GT[:], ALU.add)
                ins.then_inc(sems["gadd"], 1)

            def unit(v, kind, u, before, after):
                if u % NT == 0:
                    which, h = (kind, u // NT - 1) if u else (before, H1 - 1)
                    close(v, which, h)

            def close(v, which, h):
                if which == 2:
                    add_head(v, h)
                elif which == 1:
                    v.tally("head").add(1)

            def end(v, kind):
                close(v, kind, H1 - 1)

            pool.wait_ge(sems["primed1"], 1)
            passes(pool, dict(stats=stats, mix_values=mix_values, product_out2=lambda v, j, b: v.tally("x4").add(j == NT - 1)),
                   unit, None, end)


def build(nc, x, wqkv_t, wo_t, wr_t, w_gu, w_dn, ws_gu, ws_dn, l1w, out):
    names = sorted(PER_BATCH) + sorted(PER_EXPERT) + sorted(PER_BATCH_1) + ["loaded", "made", "slots_seen", "filled", "slots_in", "slots_f", "slots_t", "slots_i", "loaded1", "primed1"] \
        + [f"weights_in{u}" for u in range(UN)] + [f"rows_in{u}" for u in range(UN)]
    with ExitStack() as top:
        sems = {n: top.enter_context(nc.semaphore(n)) for n in names}

        def const(name, shape, dt=F32):
            return top.enter_context(nc.sbuf_tensor(name, shape, dt))

        row_d = nc.dram_tensor("rows", [T + CAP, ROW], F32, kind="Internal").ap()
        acc_d = nc.dram_tensor("stream", [T + CAP, D], F32, kind="Internal").ap()
        slot_d = nc.dram_tensor("slot_tokens", [SLOTS + NT * K * P, 1], U32, kind="Internal").ap()

        def by_batch(t):
            return t.rearrange("(b j p) d -> b p j d", b=B, p=P)

        x_b = x.rearrange("b (j p) d -> b p j d", p=P)

        ident = const("ident", [P, P])
        strict = const("strict", [P, P], BF16)
        ones16 = const("ones16", [P, P], BF16)
        onesf = const("onesf", [P, P])
        with ExitStack() as one:
            def sb(name, shape, dt=F32):
                return one.enter_context(nc.sbuf_tensor(name, shape, dt))

            def ps(name, shape, dt=F32):
                return one.enter_context(nc.psum_tensor(name, shape, dt))

            cst = dict(
                ident=ident, strict=strict, ones16=ones16, onesf=onesf,
                selq=sb("selq", [P, P], F32R), mhalf=sb("mhalf", [P, NT]),
                wqkv=sb("wqkv", [P, DC, 3 * D]), wo=sb("wo", [P, DC, D]), wrt=sb("wrt", [P, DC, E]),
                wgu=sb("wgu", [P, DC, 2 * F]), wdn=sb("wdn", [P, 2, D]),
                eoff=sb("eoff", [P, E]), dum=sb("dum", [P, 1]), koff=sb("koff", [P, NT * K]),
            )
            TIDF0 = sb("TIDF0", [P, NT])
            setup(nc, sems, sb, cst, TIDF0, (wqkv_t, wo_t, wr_t, ws_gu, ws_dn), (row_d, acc_d, slot_d))
            stage_one(nc, sems, sb, ps, (x_b, by_batch(row_d[0:T, 0:D]), by_batch(row_d[0:T, D:ROW]),
                                           by_batch(acc_d[0:T, :]), slot_d), cst, TIDF0)
        with ExitStack() as two:
            stage_two(nc, sems, lambda n, sh, dt=F32: two.enter_context(nc.sbuf_tensor(n, sh, dt)),
                      lambda n, sh, dt=F32: two.enter_context(nc.psum_tensor(n, sh, dt)),
                      (row_d, acc_d, slot_d, w_gu, w_dn), ident)
        with ExitStack() as three:
            stage_three(nc, sems, lambda n, sh, dt=F32: three.enter_context(nc.sbuf_tensor(n, sh, dt)),
                        lambda n, sh, dt=F32: three.enter_context(nc.psum_tensor(n, sh, dt)),
                        (by_batch(acc_d[0:T, :]), out.rearrange("b (j p) d -> b p j d", p=P)), l1w, ident)


def setup(nc, sems, sb, cst, tidf, weights, dram):
    wqkv_t, wo_t, wr_t, ws_gu, ws_dn = weights
    row_d, acc_d, slot_d = dram
    made = sems["made"]
    ident, strict = cst["ident"], cst["strict"]
    with ExitStack() as own:
        zero = own.enter_context(nc.sbuf_tensor("zero", [P, ROW], F32))
        selw = own.enter_context(nc.sbuf_tensor("selw", [P, P], F32))
        none = own.enter_context(nc.sbuf_tensor("none", [E, CAP], U32))
        numi = own.enter_context(nc.sbuf_tensor("numi", [P, NT + E + 1 + NT * K], I32))
        with nc.Block() as block:
            @block.sync
            def _(sp):
                loads = [
                    (cst["wqkv"][:], wqkv_t.rearrange("(c p) n -> p c n", p=P)),
                    (cst["wo"][:], wo_t.rearrange("(c p) n -> p c n", p=P)),
                    (cst["wrt"][:], wr_t.rearrange("(c p) n -> p c n", p=P)),
                    (cst["wgu"][:], ws_gu.rearrange("(c p) n -> p c n", p=P)),
                    (cst["wdn"][:, 0, :], ws_dn[0:P, :]),
                    (cst["wdn"][P - FC:P, 1, :], ws_dn[P:F, :]),
                ]
                for dst, src in loads:
                    sp.dma_start(dst, src).then_inc(sems["loaded"], 16)
                sp.wait_ge(made, 9)
                sp.dma_start(row_d[T:, :], zero[:]).then_inc(sems["filled"], 16)
                sp.dma_start(acc_d[T:, :], zero[:, 0:D]).then_inc(sems["filled"], 16)
                sp.dma_start(slot_d[0:SLOTS, 0].rearrange("(e s) -> e s", e=E), none[:]).then_inc(sems["filled"], 16)
                sp.wait_ge(sems["loaded"], 16 * len(loads))
                sp.wait_ge(sems["filled"], 48)

            @block.gpsimd
            def _(pool):
                pool.memset(ident[:], 0.0)
                pool.memset(strict[:], 1.0)
                pool.memset(selw[:], 0.0)
                pool.memset(cst["ones16"][:], 1.0)
                pool.memset(cst["onesf"][:], 1.0)
                pool.memset(zero[:], 0.0)
                pool.memset(cst["mhalf"][:], -0.5)
                pool.drain()
                pool.affine_select(out=ident[:], in_=ident[:], compare_op=ALU.not_equal, fill=1.0, base=0,
                                   pattern=[[-1, P]], channel_multiplier=1).then_inc(made, 1)
                pool.affine_select(out=strict[:], in_=strict[:], compare_op=ALU.is_gt, fill=0.0, base=0,
                                   pattern=[[1, P]], channel_multiplier=-1).then_inc(made, 1)
                for r in (DH0, DH0 + 2 * QV, SL + DH0, SL + DH0 + 2 * QV):
                    ins = pool.affine_select(out=selw[:], in_=selw[:], compare_op=ALU.not_equal, fill=1.0,
                                             base=-r, pattern=[[0, P]], channel_multiplier=1)
                    pool.drain()
                ins.then_inc(made, 1)
                pool.iota(none[:], [[1, CAP]], base=T, channel_multiplier=0).then_inc(made, 1)
                pool.iota(numi[:, 0:NT], [[P, NT]], base=0, channel_multiplier=1).then_inc(made, 1)
                pool.iota(numi[:, NT:NT + E], [[CAP, E]], base=1, channel_multiplier=0).then_inc(made, 1)
                pool.iota(numi[:, NT + E:NT + E + 1], [[0, 1]], base=SLOTS + 1, channel_multiplier=1).then_inc(made, 1)
                pool.iota(numi[:, NT + E + 1:], [[P, NT * K]], base=0, channel_multiplier=0).then_inc(made, 1)
                pool.drain()
                pool.sem_inc(made, 1)

            @block.vector
            def _(dve):
                dve.wait_ge(made, 9)
                dve.tensor_copy(cst["selq"][:], selw[:])
                dve.tensor_copy(tidf[:], numi[:, 0:NT])
                dve.tensor_copy(cst["eoff"][:], numi[:, NT:NT + E])
                dve.tensor_copy(cst["dum"][:], numi[:, NT + E:NT + E + 1])
                dve.tensor_copy(cst["koff"][:], numi[:, NT + E + 1:])


def kernel(**inputs):
    import concourse.bacc as _bacc
    from concourse.bass_utils import run_bass_kernel_spmd as _run

    a = {k: np.asarray(v) for k, v in inputs.items()}
    arrays = dict(
        x=a["L0_attn_x"],
        wqkv_t=np.concatenate([a["L0_attn_wq"].T, a["L0_attn_wk"].T, a["L0_attn_wv"].T], axis=1),
        wo_t=a["L0_attn_wo"].T,
        wr_t=a["L0_ffn_router_w"].T,
        w_gu=np.concatenate([a["L0_ffn_w_gate"], a["L0_ffn_w_up"]], axis=2),
        w_dn=a["L0_ffn_w_down"],
        ws_gu=a["L0_ffn_ws_gate_up"],
        ws_dn=a["L0_ffn_ws_down"],
        q1=a["L1_attn_Wq"].T, down1=a["L1_attn_Wkv_down"].T, k1=a["L1_attn_Wk_up"].T, v1=a["L1_attn_Wv_up"].T,
        o1=a["L1_attn_Wo"].T,
        q2=a["L1_ffn_Wq"], k2=a["L1_ffn_Wk"], g2=np.concatenate([a["L1_ffn_Ws"], a["L1_ffn_Wd"]], axis=1),
        v2=a["L1_ffn_Wv"].transpose(1, 0, 2).reshape(D, SV), o2=a["L1_ffn_Wo"].reshape(SV, D),
    )
    arrays = {k: np.ascontiguousarray(v) for k, v in arrays.items()}
    nc = _bacc.Bacc("TRN2", target_bir_lowering=False, num_devices=1)
    args = {k: nc.dram_tensor(k, list(v.shape), mybir.dt.from_np(v.dtype), kind="ExternalInput").ap()
            for k, v in arrays.items()}
    l1w = {k: args.pop(k) for k in list(args) if k[-1] in "12"}
    out = nc.dram_tensor("out", [B, N, D], F32, kind="ExternalOutput").ap()
    build(nc, *args.values(), l1w, out)
    r = _run(nc, [arrays], core_ids=[0])
    return r.results[0]["out"]
```
